# Optimizing a Trainium2 kernel written in Bass

```python
import numpy as np
import jax
import jax.numpy as jnp

def _softmax(x, axis=-1):
    return jax.nn.softmax(x, axis=axis)

def _gelu(x):
    return jax.nn.gelu(x, approximate=True)

def _silu(x):
    return jax.nn.silu(x)

def _sigmoid(x):
    return jax.nn.sigmoid(x)

def _layernorm(x, axis=-1, eps=1e-05):
    m = jnp.mean(x, axis=axis, keepdims=True)
    v = jnp.var(x, axis=axis, keepdims=True)
    return (x - m) / jnp.sqrt(v + eps)

def _scatter_add(tgt, idx, src, axis=0):
    return tgt.at[idx].add(src)

def _segment_sum(src, seg, n):
    return jax.ops.segment_sum(src, seg, n)
kernel_name = 'mk_early_fusion_d1_tok_img768_r4_77599b'

def setup_inputs(seed: int=0):
    np.random.seed(seed)
    _w = jnp.asarray

    def _rec_inputs():
        import jax
        import jax.numpy as jnp
        _rk = jax.random.key(seed)
        x = -0.000147625 + 0.999875 * jax.random.normal(jax.random.fold_in(_rk, 1), (64, 12, 224, 224), jnp.float32)
        txt = -0.0221329 + 10 * jax.random.normal(jax.random.fold_in(_rk, 2), (64, 128, 192), jnp.float32)
        return (x, txt)
    x, txt = _rec_inputs()

    def _L0_tok_setup():
        import jax, jax.numpy as jnp
        import numpy as np
        IMG = 224
        PATCH = 16
        EMBED = 192
        C = 12
        B = 64
        key = jax.random.key(seed)
        k1, k2 = jax.random.split(key)
        x = jax.random.normal(k1, (B, C, IMG, IMG), dtype=jnp.float32)
        channel_weights = jax.random.normal(k2, (C, EMBED), dtype=jnp.float32)
        return {'x': x, 'channel_weights': channel_weights}
    _L0_tok_all = _L0_tok_setup()
    _L0_tok_in = {k: v for k, v in _L0_tok_all.items() if k in ('channel_weights',)}
    del _L0_tok_all

    def _L0_attn_setup():
        import jax, jax.numpy as jnp
        import numpy as np
        B, L, D_MODEL = (2, 1024, 192)
        D_STATE, D_CONV, EXPAND = (16, 4, 2)
        E = EXPAND * D_MODEL
        LN_EPS = 1e-05
        key = jax.random.key(seed)
        ks = jax.random.split(key, 8)
        s = lambda k, shape, scale: jax.random.normal(k, shape, jnp.float32) * scale
        return {'x': jax.random.normal(ks[0], (B, L, D_MODEL), jnp.float32), 'ln_g': jnp.ones((D_MODEL,), jnp.float32), 'ln_b': jnp.zeros((D_MODEL,), jnp.float32), 'W_in': s(ks[1], (D_MODEL, E), 0.02), 'b_in': jnp.zeros((E,), jnp.float32), 'W_conv': s(ks[2], (E, 1, D_CONV), 0.1), 'b_conv': jnp.zeros((E,), jnp.float32), 'W_xp': s(ks[3], (E, D_STATE + D_MODEL), 0.02), 'b_xp': jnp.zeros((D_STATE + D_MODEL,), jnp.float32), 'W_dt': s(ks[4], (E, D_STATE), 0.02), 'b_dt': jnp.zeros((D_STATE,), jnp.float32), 'W_us': s(ks[5], (D_STATE, D_MODEL), 0.02), 'b_us': jnp.zeros((D_MODEL,), jnp.float32), 'W_out': s(ks[6], (E, D_MODEL), 0.02), 'b_out': jnp.zeros((D_MODEL,), jnp.float32)}
    _L0_attn_all = _L0_attn_setup()
    _L0_attn_in = {k: v for k, v in _L0_attn_all.items() if k in ('ln_g', 'ln_b', 'W_in', 'b_in', 'W_conv', 'b_conv', 'W_xp', 'b_xp', 'W_dt', 'b_dt', 'W_us', 'b_us', 'W_out', 'b_out')}
    del _L0_attn_all

    def _L0_ffn_setup():
        import jax, jax.numpy as jnp
        import numpy as np
        B, S, D = (4, 256, 192)
        E = 8
        H = 192
        HS = 768
        TOPK_ROUTED = 2
        key = jax.random.key(seed)
        ks = jax.random.split(key, 10)
        w = lambda k, shape: jax.random.normal(k, shape, dtype=jnp.float32) * 0.02
        return {'x': jax.random.normal(ks[0], (B, S, D), dtype=jnp.float32), 'router_w': w(ks[1], (D, E)), 'w_gate': w(ks[2], (E, D, H)), 'w_up': w(ks[3], (E, D, H)), 'w_down': w(ks[4], (E, H, D)), 'ws_gate': w(ks[5], (D, HS)), 'ws_up': w(ks[6], (D, HS)), 'ws_down': w(ks[7], (HS, D)), 'sg_w': w(ks[8], (D, 1)), 'sg_b': jnp.zeros((1,), jnp.float32)}
    _L0_ffn_all = _L0_ffn_setup()
    _L0_ffn_in = {k: v for k, v in _L0_ffn_all.items() if k in ('router_w', 'w_gate', 'w_up', 'w_down', 'ws_gate', 'ws_up', 'ws_down', 'sg_w', 'sg_b')}
    del _L0_ffn_all
    return {'x': x, 'txt': txt, 'L0_tok_channel_weights': _L0_tok_in['channel_weights'], 'L0_attn_ln_g': _L0_attn_in['ln_g'], 'L0_attn_ln_b': _L0_attn_in['ln_b'], 'L0_attn_W_in': _L0_attn_in['W_in'], 'L0_attn_b_in': _L0_attn_in['b_in'], 'L0_attn_W_conv': _L0_attn_in['W_conv'], 'L0_attn_b_conv': _L0_attn_in['b_conv'], 'L0_attn_W_xp': _L0_attn_in['W_xp'], 'L0_attn_b_xp': _L0_attn_in['b_xp'], 'L0_attn_W_dt': _L0_attn_in['W_dt'], 'L0_attn_b_dt': _L0_attn_in['b_dt'], 'L0_attn_W_us': _L0_attn_in['W_us'], 'L0_attn_b_us': _L0_attn_in['b_us'], 'L0_attn_W_out': _L0_attn_in['W_out'], 'L0_attn_b_out': _L0_attn_in['b_out'], 'L0_ffn_router_w': _L0_ffn_in['router_w'], 'L0_ffn_w_gate': _L0_ffn_in['w_gate'], 'L0_ffn_w_up': _L0_ffn_in['w_up'], 'L0_ffn_w_down': _L0_ffn_in['w_down'], 'L0_ffn_ws_gate': _L0_ffn_in['ws_gate'], 'L0_ffn_ws_up': _L0_ffn_in['ws_up'], 'L0_ffn_ws_down': _L0_ffn_in['ws_down'], 'L0_ffn_sg_w': _L0_ffn_in['sg_w'], 'L0_ffn_sg_b': _L0_ffn_in['sg_b']}

def reference(x, txt, L0_tok_channel_weights, L0_attn_ln_g, L0_attn_ln_b, L0_attn_W_in, L0_attn_b_in, L0_attn_W_conv, L0_attn_b_conv, L0_attn_W_xp, L0_attn_b_xp, L0_attn_W_dt, L0_attn_b_dt, L0_attn_W_us, L0_attn_b_us, L0_attn_W_out, L0_attn_b_out, L0_ffn_router_w, L0_ffn_w_gate, L0_ffn_w_up, L0_ffn_w_down, L0_ffn_ws_gate, L0_ffn_ws_up, L0_ffn_ws_down, L0_ffn_sg_w, L0_ffn_sg_b):
    import jax
    import jax.numpy as jnp

    def _L0_tok_ref(x, channel_weights):
        import jax, jax.numpy as jnp
        import numpy as np
        IMG = 224
        PATCH = 16
        EMBED = 192
        C = 12
        B = 64
        Bb, Cc, H, W = x.shape
        K = PATCH
        n = H // K
        pooled = x.reshape(Bb, Cc, n, K, n, K).sum(axis=(3, 5))
        out = jnp.einsum('bcij,ce->bije', pooled, channel_weights)
        return out.reshape(Bb, n * n, EMBED)

    def _L0_attn_ref(x, ln_g, ln_b, W_in, b_in, W_conv, b_conv, W_xp, b_xp, W_dt, b_dt, W_us, b_us, W_out, b_out):
        import jax, jax.numpy as jnp
        import numpy as np
        B, L, D_MODEL = (2, 1024, 192)
        D_STATE, D_CONV, EXPAND = (16, 4, 2)
        E = EXPAND * D_MODEL
        LN_EPS = 1e-05
        Bsz, Ls, Dm = x.shape
        mu = jnp.mean(x, axis=-1, keepdims=True)
        var = jnp.mean((x - mu) ** 2, axis=-1, keepdims=True)
        xn = (x - mu) * jax.lax.rsqrt(var + LN_EPS) * ln_g + ln_b
        x_in = xn @ W_in + b_in
        xc = jnp.transpose(x_in, (0, 2, 1))
        xc = jax.lax.conv_general_dilated(xc, W_conv, window_strides=(1,), padding=[(D_CONV - 1, 0)], dimension_numbers=('NCH', 'OIH', 'NCH'), feature_group_count=E) + b_conv[None, :, None]
        x_act = jax.nn.silu((jnpp := jnp.transpose(xc, (0, 2, 1))))
        xd = x_act @ W_xp + b_xp
        xs, ds = (xd[..., :Dm], xd[..., Dm:])
        dt = jax.nn.softplus(x_act @ W_dt + b_dt)
        a = jnp.exp(-dt)
        bterm = ds * jnp.exp(-dt / 2)

        def step(carry, ab):
            at, bt = ab
            v = at * carry + bt
            return (v, v)
        _, v = jax.lax.scan(step, jnp.zeros((Bsz, dt.shape[-1]), x.dtype), (jnp.swapaxes(a, 0, 1), jnp.swapaxes(bterm, 0, 1)))
        v = jnp.swapaxes(v, 0, 1)
        k = jnp.arange(Ls - 1, -1, -1, dtype=x.dtype)[None, :, None]
        denom = jnp.expm1(-dt)
        denom = jnp.where(denom > -1e-30, -1e-30, denom)
        us = jnp.exp(-k * dt) * v + bterm * jnp.expm1(-k * dt) / denom
        y = xs + us @ W_us + b_us
        y = jnp.concatenate([y, x_act[..., Dm:]], axis=-1) @ W_out + b_out
        return y

    def _L0_ffn_ref(x, router_w, w_gate, w_up, w_down, ws_gate, ws_up, ws_down, sg_w, sg_b):
        import jax, jax.numpy as jnp
        import numpy as np
        B, S, D = (4, 256, 192)
        E = 8
        H = 192
        HS = 768
        TOPK_ROUTED = 2
        probs = jax.nn.softmax(x @ router_w, axis=-1)
        gates, idx = jax.lax.top_k(probs, TOPK_ROUTED)
        gates = gates / jnp.sum(gates, axis=-1, keepdims=True)
        n_exp = router_w.shape[1]
        dense_g = jnp.sum(jax.nn.one_hot(idx, n_exp, dtype=x.dtype) * gates[..., None], axis=-2)
        g = jax.nn.silu(jnp.einsum('bsd,edh->bseh', x, w_gate))
        u = jnp.einsum('bsd,edh->bseh', x, w_up)
        expert_out = jnp.einsum('bseh,ehd->bsed', g * u, w_down)
        routed = jnp.einsum('bse,bsed->bsd', dense_g, expert_out)
        shared = jax.nn.silu(x @ ws_gate) * (x @ ws_up) @ ws_down
        alpha = jax.nn.sigmoid(x @ sg_w + sg_b)
        return alpha * shared + (1.0 - alpha) * routed
    h = _L0_tok_ref(x, L0_tok_channel_weights)
    h = jnp.concatenate([h, txt], axis=1)
    h = h + _L0_attn_ref(_layernorm(h, axis=-1), L0_attn_ln_g, L0_attn_ln_b, L0_attn_W_in, L0_attn_b_in, L0_attn_W_conv, L0_attn_b_conv, L0_attn_W_xp, L0_attn_b_xp, L0_attn_W_dt, L0_attn_b_dt, L0_attn_W_us, L0_attn_b_us, L0_attn_W_out, L0_attn_b_out)
    h = h + _L0_ffn_ref(_layernorm(h, axis=-1), L0_ffn_router_w, L0_ffn_w_gate, L0_ffn_w_up, L0_ffn_w_down, L0_ffn_ws_gate, L0_ffn_ws_up, L0_ffn_ws_down, L0_ffn_sg_w, L0_ffn_sg_b)
    return h

_drawn_inputs = setup_inputs


def setup_inputs(seed=0):
    import zlib

    import numpy as np

    out = dict(_drawn_inputs(seed))
    spreads = {'L0_attn_ln_g': (1.0, 0.6),
     'L0_attn_ln_b': (0.0, 0.8),
     'L0_attn_b_in': (0.0, 0.8),
     'L0_attn_b_conv': (0.0, 0.8),
     'L0_attn_b_xp': (0.0, 0.8),
     'L0_attn_b_dt': (0.0, 0.8),
     'L0_attn_b_us': (0.0, 2.0),
     'L0_attn_b_out': (0.0, 2.0)}
    factors = {'L0_attn_W_in': 8.0,
     'L0_attn_W_conv': 8.0,
     'L0_attn_W_xp': 8.0,
     'L0_attn_W_dt': 8.0,
     'L0_attn_W_us': 8.0,
     'L0_attn_W_out': 8.0,
     'L0_ffn_router_w': 64.0,
     'L0_ffn_w_gate': 64.0,
     'L0_ffn_w_up': 64.0,
     'L0_ffn_w_down': 64.0,
     'L0_ffn_ws_gate': 64.0,
     'L0_ffn_ws_up': 64.0,
     'L0_ffn_ws_down': 64.0,
     'L0_ffn_sg_w': 64.0}
    for name, (base, spread) in spreads.items():
        noise = np.random.default_rng([zlib.crc32(name.encode()), seed]).standard_normal(out[name].shape)
        drawn = base * np.exp(spread * noise) if base else spread * noise
        out[name] = jnp.asarray(drawn.astype(out[name].dtype))
    for name, factor in factors.items():
        out[name] = (out[name] * factor).astype(out[name].dtype)
    return out
```

```python
from contextlib import ExitStack

import concourse.bass as bass
from concourse import mybir

F32 = mybir.dt.float32
F32R = mybir.dt.float32r
U32 = mybir.dt.uint32
ALU = mybir.AluOpType
ACT = mybir.ActivationFunctionType
AX_X = mybir.AxisListType.X

P = 128
SLOTS = 36
RING = 7
CHUNKS = 21


PE_STEPS = (
    "pool:0 gate up down",
    "gate up down",
    "gate us:1:0 us:1:1 up down",
    "gate up down",
    "gate mixA:0 mixC:0 up down",
    "gate up pool:1 in:0:0 down",
    "gate up down",
    "gate up in:0:1 in:0:2 down",
    "gate up down mlpA:1",
    "gate up down",
    "gate up down mlpC:1",
    "gate up mixA:1 down",
    "gate up mixC:1 down",
    "gate in:1:0 route:1 up down",
    "gate up act:0:0 act:0:1 in:1:1 down in:1:2",
    "gate up gates:1 down",
    "gate up down",
    "gate up down act:1:0 act:1:1",
    "gate up down",
    "gate up dt down",
    "gate ds up down",
    "gate up down",
    "gate up down",
    "gate up down",
    "gate up down",
    "gate up down",
    "gate up us:0:0 us:0:1 down",
    "gate up down",
    "gate up down",
    "gate mlpA:0 mlpC:0 up down",
    "gate route:0 up down",
    "gate up down",
    "gate up down gates:0",
    "gate up down",
    "gate up down",
    "gate up down",
)
ACT_STEPS = (
    "pool:0 silu hi",
    "silu hi",
    "silu hi",
    "silu double:0 hi",
    "silu mixC:0 hi mixA:0",
    "silu hi in:0:0",
    "silu pool:1 hi",
    "silu hi convsilu:0:0 in:0:1 in:0:2",
    "silu doublef:1 hi",
    "silu hi",
    "silu hi mlpA:1 double:1 mlpC:1",
    "silu hi mixA:1 convsilu:0:1 convsilu:0:2",
    "silu mixC:1 hi",
    "silu in:1:0 hi",
    "silu gtanh:1 hi act:0:0 act:0:1 in:1:1 in:1:2",
    "silu convsilu:1:0 hi gates:1 convsilu:1:1",
    "silu hi convsilu:1:2",
    "silu act:1:0 hi",
    "silu act:1:1 hi",
    "silu dt hi",
    "silu exp ln hi exp2 ds",
    "silu hi tanh",
    "silu hi",
    "silu hi",
    "silu hi",
    "silu states hi",
    "silu hi",
    "silu hi",
    "silu doublef:0 hi",
    "silu mlpC:0 mlpA:0 hi",
    "silu hi",
    "silu gtanh:0 hi",
    "silu hi gates:0",
    "silu hi",
    "silu hi",
    "silu hi",
)
DVE_STEPS = (
    "hidden stats:0 lo",
    "hidden lo result:1",
    "hidden norm:0 lo",
    "hidden us:1:0 lo us:1:1 statsf:1",
    "hidden mixC:0 lo mixA:0",
    "hidden normf:1 pool:0 pool:1 lo",
    "hidden conv:0:0 lo",
    "hidden pool:2 lo stats:1 conv:0:1",
    "hidden norm:1 lo",
    "hidden lo",
    "hidden conv:0:2 lo mlpA:1",
    "hidden lo",
    "hidden mlpC:1 actlo:0:0 mixA:1 pool:3 mixC:1 pool:4 pool:5 lo",
    "hidden route:1 actlo:0:1 actlo:0:2 lo",
    "hidden pick:1 weigh:1 lo conv:1:0",
    "hidden conv:1:1 conv:1:2 lo pool:6",
    "hidden actlo:1:0 lo actlo:1:1 actlo:1:2 pool:7 pool:8 pool:9",
    "hidden lo pool:10 pool:11",
    "hidden lo",
    "hidden pool:12 pool:13 result:0 pool:14 lo",
    "hidden softplus:0 softplus:1 lo",
    "hidden lo scan:0",
    "hidden scan:1 lo",
    "hidden pool:15 lo",
    "hidden scan:2 lo scan:3",
    "hidden stateslo lo",
    "hidden us:0:0 us:0:1 lo",
    "hidden statsf:0 lo normf:0",
    "hidden lo",
    "hidden mlpC:0 mlpA:0 lo",
    "hidden lo",
    "hidden route:0 pick:0 pool:16 lo weigh:0",
    "hidden lo",
    "hidden lo",
    "hidden pool:17 pool:18 pool:19 lo pool:20",
    "hidden lo",
)
POOL_STEPS = (
    "gated",
    "gated rstd:0",
    "gated",
    "gated",
    "gated rstdf:1",
    "gated",
    "gated",
    "gated rstd:1",
    "gated",
    "gated",
    "gated",
    "gated",
    "gated",
    "gated",
    "gated",
    "gated addy:0:0",
    "gated",
    "gated addy:0:1 addy:1:0 addy:1:1",
    "gated",
    "gated",
    "gated scanin",
    "gated",
    "gated",
    "gated",
    "gated",
    "gated",
    "gated rstdf:0",
    "gated",
    "gated",
    "gated",
    "gated",
    "gated",
    "gated",
    "gated",
    "gated",
    "gated",
)
SP_STEPS = (
    "text:1 load:0 load:1 load:2 load:3 load:4 load:5 gates:1 load:6 load:7 load:8 load:9 store:1 store:0 load:10 load:11 load:12 load:13 text:0 load:14 load:15 gates:0 load:16 load:17 load:18 load:19 load:20",
)

TAIL = ("us", "statsf", "rstdf", "normf", "doublef", "mlpA", "mlpC", "route", "pick", "gtanh", "weigh", "gates")

def build(nc, x, txt, cw, ln_g, ln_b, W_in, b_in, W_conv, b_conv, W_xp, b_xp, W_dt, b_dt, W_us, b_us,
          W_out, b_out, router_w, w_gate, w_up, w_down, ws_gate, ws_up, ws_down, sg_w, sg_b, out):
    B, C, HW, _ = x.shape
    D = cw.shape[1]
    PATCH = 16
    G = HW // PATCH
    IMG = G * G
    L = out.shape[1]
    TM = L // 3
    E1 = W_in.shape[1]
    KE = E1 // P
    NST = W_dt.shape[1]
    NX = D + 2 * NST
    R = D - P
    NE = router_w.shape[1]
    RT = NE * w_gate.shape[2] // P
    ST = ws_gate.shape[1] // P
    T = RT + ST
    NP = B // 2
    CH = 2 * G * PATCH
    EPS = 1e-5
    assert 3 * TM == L and L - IMG == txt.shape[1] and 2 * T == SLOTS and NP >= 5 and C == 12

    x_rows = x.rearrange("b c h w -> (b c) h w")
    routed_gates_dram = nc.dram_tensor("routed_gates", [16, L], F32).ap()

    ctx = ExitStack()
    with ctx:
        def sb(name, shape, dt=F32):
            return ctx.enter_context(nc.sbuf_tensor(name, shape, dt))

        def sem(name):
            return ctx.enter_context(nc.semaphore(name))

        upA_hi = sb("upA_hi", [P, 2 * T * P], F32R)
        upA_lo = sb("upA_lo", [P, 2 * T * P], F32R)
        upC_hi = sb("upC_hi", [P, 2 * T * P], F32R)
        upC_lo = sb("upC_lo", [P, 2 * T * P], F32R)
        down = sb("down", [P, T, 2 * D], F32R)
        inA_hi = sb("inA_hi", [P, E1], F32R)
        inA_lo = sb("inA_lo", [P, E1], F32R)
        inC_hi = sb("inC_hi", [P, E1], F32R)
        inC_lo = sb("inC_lo", [P, E1], F32R)
        actw_hi = sb("actw_hi", [P, KE, NX], F32R)
        actw_lo = sb("actw_lo", [P, KE, NX], F32R)
        usw = sb("usw", [P, 2, D], F32R)
        routeA = sb("routeA", [P, 32], F32R)
        routeC = sb("routeC", [P, 32], F32R)
        chan = sb("chan", [P, 4, D])
        ident = sb("ident", [P, P])
        taps = sb("taps", [P, KE, 4])
        col = sb("col", [P, 24])
        lnb = sb("lnb", [P, 4])
        biota = sb("biota", [P, NE])
        khalf = sb("khalf", [32, L])
        power = sb("power", [P, 3])
        ring = sb("ring", [P, RING, CH])
        pooled = sb("pooled", [P, 3, IMG])
        h = sb("h", [P, 2, 3, D])
        hf = sb("hf", [P, 2, 3, D])
        res = sb("res", [P, 3, D])
        stats = sb("stats", [P, 4, 3, 6])
        mv = sb("mv", [P, 4, 3, 2])
        rstd = sb("rstd", [P, 4, 3])
        xn = sb("xn", [P, 3, 2 * P])
        xnf = sb("xnf", [P, 3, 2 * P])
        mixA_hi = sb("mixA_hi", [P, L], F32R)
        mixA_lo = sb("mixA_lo", [P, L], F32R)
        mixC = sb("mixC", [P, L], F32R)
        mlpA_hi = sb("mlpA_hi", [P, 2, L], F32R)
        mlpA_lo = sb("mlpA_lo", [P, 2, L], F32R)
        mlpC = sb("mlpC", [P, 2, L], F32R)
        xin = sb("xin", [P, KE, 3 + L])
        conv = sb("conv", [P, KE, L])
        act_hi = sb("act_hi", [P, KE, L], F32R)
        act_lo = sb("act_lo", [P, KE, L], F32R)
        yz = sb("yz", [P, 3, NX])
        zs = sb("zs", [P, 3, 4 * NST])
        xn_st, yz_st = (a[0:32, :, :].rearrange("p m d -> p (m d)") for a in (xn, yz))
        sc = [conv[0:32, 0, :], conv[0:32, 1, :], conv[0:32, 2, :], xn_st[:, 0:L], xn_st[:, L:2 * L], yz_st[:, 0:L],
              yz_st[:, L:2 * L]]
        us = sb("us", [P, L], F32R)
        lg = sb("lg", [P, 3, 32])
        logit = sb("logit", [P, 3, 16])
        top = sb("top", [P, 3, 8])
        topi = sb("topi", [P, 3, 8], U32)
        topf = sb("topf", [P, 3, 8])
        gsc = sb("gsc", [P, 8, 3])
        pick = sb("pick", [P, 2, 3, 8])
        gt = sb("gt", [P, 3, 9])
        gs = sb("gs", [9, L])
        gate_bc = sb("gate_bc", [P, NE, L])
        alpha_bc = sb("alpha_bc", [P, 2, L])
        hid = sb("hid", [P, 3, L])
        hid_hi = sb("hid_hi", [P, 3, L], F32R)
        hid_lo = sb("hid_lo", [P, 3, L], F32R)
        gb_flat = gate_bc[:, :, :].rearrange("p e l -> p (e l)")
        STG = 4 * D
        stage = [gb_flat[:, STG * k:STG * (k + 1)] for k in range(3)]
        hf_flat = hf[:, :, :, :].rearrange("p b m d -> p (b m d)")
        win_st = [hf_flat[:, 0:E1], hf_flat[:, E1:2 * E1]]
        wout_st = [hf_flat[:, 2 * E1:2 * E1 + D], hf_flat[0:R, 2 * E1 + D:2 * E1 + 2 * D]]
        hid_flat = hid[:, :, :].rearrange("p s l -> p (s l)")
        wxp_st = hid_flat[:, 0:KE * (D + NST)].rearrange("p (k n) -> p k n", k=KE)
        wdt_st = hid_flat[:, KE * (D + NST):KE * NX].rearrange("p (k n) -> p k n", k=KE)
        wus_st = hid_flat[0:NST, KE * NX:KE * NX + D]
        woutf_st = res
        xnf_flat = xnf[:, :, :].rearrange("p m d -> p (m d)")
        wxpT = [xnf_flat[:, 0:E1], xnf_flat[0:R, E1:2 * E1]]
        al_flat = alpha_bc[:, :, :].rearrange("p b l -> p (b l)")
        uslT = [al_flat[:, 0:2 * P].rearrange("p (b c) -> p b c", b=2),
                al_flat[0:R, 2 * P:4 * P].rearrange("p (b c) -> p b c", b=2)]
        xn_flat = xn[:, :, :].rearrange("p m d -> p (m d)")
        bout_st = xn_flat[:, 0:D]
        uw = xn_flat[:, D:2 * D]
        rt_st = sb("rt_st", [P, 2, 16])
        wx_full = yz
        iota_i = conv[:, 0, :].bitcast(mybir.dt.int32)
        settled = sb("settled", [1, 1])
        binf = sb("binf", [P, KE])
        bconv = sb("bconv", [P, KE])
        sgbh = sb("sgbh", [P, 1])

        GA, GC, BIN, BCV, BDT, BDS, SGB, MHI, MLO = 0, 1, 4, 7, 13, 14, 15, 16, 17
        USC, XPC = 18, 20

        gu = ctx.enter_context(nc.psum_tensor("gu", [P, 3, 512], F32))
        acc = ctx.enter_context(nc.psum_tensor("acc", [P, 3, 512], F32))
        misc = ctx.enter_context(nc.psum_tensor("misc", [P, 2, 512], F32))
        prep = misc[:, 0, :]

        s_small = sem("small_weights_loaded")
        s_zeroed = sem("zeroed_for_loads")
        s_const = sem("constants_made")
        s_const_chain = sem("constants_chain")
        s_stage = [sem(f"stage_loaded{k}") for k in range(3)]
        s_stage_hi = sem("stage_hi_split")
        s_stage_lo = sem("stage_lo_split")
        s_prep_pe = sem("prep_products")
        s_prep_act = sem("prep_evacuated")
        s_prep_dve = sem("prep_vector_chain")
        s_usl = sem("state_weights_stacked")
        s_prep_w = sem("mixer_weights_ready")
        s_chunk = [sem(f"chunk_loaded{k}") for k in range(RING)]
        s_pooled = sem("chunk_pooled")
        s_txt = [sem(f"text_loaded{b}") for b in range(2)]
        s_job = {k: sem(f"{k}_product") for k in ("pool", "mixA", "mixC", "in", "act", "dt", "ds", "us", "mlpA", "mlpC",
                                                  "route", "gates")}
        s_tokens = sem("tokens_in_h")
        s_stat = sem("stats_chain")
        s_mv = sem("mean_var")
        s_rstd_a = sem("variance_scaled")
        s_rstd = sem("rstd")
        s_norm = sem("normalised")
        s_dup = sem("normalised_tail_doubled")
        s_mixhi, s_mixlo, s_mixc0, s_mixc = sem("mixA_hi_ready"), sem("mixA_lo_ready"), sem("mixC_hi_ready"), sem("mixC_ready")
        s_xin = sem("conv_input_ready")
        s_tap = sem("conv_taps")
        s_silu1 = sem("mixer_silu")
        s_acthi = sem("act_hi_ready")
        s_actlo = sem("act_lo_ready")
        s_yz = sem("yz_evacuated")
        s_hy = sem("h_plus_y")
        s_zs = sem("zs_ready")
        s_dtev = sem("dt_evacuated")
        s_dsev = sem("ds_evacuated")
        s_exp1, s_ln, s_exp2, s_tanh1, s_tanhk = (sem(n) for n in ("exp_az", "ln_w", "exp_half_dt", "tanh_half_dt", "tanh_half_kdt"))
        s_scan = sem("scan_chain")
        s_scan_w = sem("scan_w")
        s_dtdone = sem("dt_ready")
        s_kd = sem("kdt_ready")
        s_ab = sem("scan_inputs")
        s_usf = sem("us_float")
        s_ushi = sem("us_hi")
        s_uslo = sem("us_lo")
        s_hf = sem("hf_ready")
        s_statf = sem("mlp_stats_chain")
        s_mvf, s_rstdf_a, s_rstdf, s_normf, s_dupf = (sem(n) for n in ("mlp_mean_var", "mlp_variance_scaled", "mlp_rstd", "mlp_normalised",
                                                                  "mlp_normalised_doubled"))
        s_mlphi, s_mlplo, s_mlpc0, s_mlpc = sem("mlpA_hi_ready"), sem("mlpA_lo_ready"), sem("mlpC_hi_ready"), sem("mlpC_ready")
        s_lg = sem("logits_evacuated")
        s_gate = sem("gates_chain")
        s_diff = sem("logit_difference")
        s_gtanh = sem("gate_tanh")
        s_gt = sem("gates_token_major")
        s_gs = sem("gates_feature_major")
        s_gdram = sem("gates_in_dram")
        s_gbc = sem("gates_loaded")
        s_g, s_u, s_sil, s_gated, s_hid, s_hi, s_lo, s_down = (sem(n) for n in (
            "gate_projected", "up_projected", "silu_done", "gated", "hidden_ready", "hidden_hi", "hidden_lo", "down_projected"))
        s_res1 = sem("result_half")
        s_res = sem("result_ready")
        s_out = sem("result_stored")

        SMALL_COUNT = 59

        block = ctx.enter_context(nc.Block())

        def wait(eng, s, value):
            if isinstance(value, int) and value <= 0:
                return
            eng.wait_ge(s, value)

        def parts(i):
            return dict(mlp=i >= 0, carry=i >= 1, mix=-1 <= i <= NP - 2, pooling=i <= NP - 3)

        def iterations(eng, body, loop_to):
            for i in (-2, -1, 0):
                body(i, **parts(i))
            with eng.Fori(1, loop_to + 1) as i:
                body(i, **parts(1))
            for i in range(loop_to + 1, NP):
                body(i, **parts(i))

        FULL = NP - 3

        def steps(table, slot):
            for word in table[slot].split():
                name, *numbers = word.split(":")
                if name == "pool" and table is DVE_STEPS or name in ("scan", "softplus", "load"):
                    numbers = [0, *numbers]
                yield (name, *(int(n) for n in numbers), *[0] * (2 - len(numbers)))

        def pair_of(i, name, b, mlp, mix):
            if name in TAIL and b == 1:
                return i if mlp else None
            return i + 1 if mix else None

        def evacuated(name, b, k, q):
            beta = 2 * q + b
            return {
                "pool": (s_tokens, beta + 1), "mixA": (s_mixlo, beta + 1), "mixC": (s_mixc, beta + 1),
                "in": (s_xin, 3 * beta + k + 1), "act": (s_yz, 2 * beta + k + 1), "dt": (s_dtev, q + 1), "ds": (s_dsev, q + 1),
                "us": (s_hf, 2 * beta + k + 1), "mlpA": (s_mlplo, beta + 1), "mlpC": (s_mlpc, beta + 1),
                "route": (s_lg, beta + 1), "gates": (s_gs, beta + 1),
            }[name]

        JOBS = [step for slot in range(SLOTS) for step in steps(PE_STEPS, slot) if step[0] not in ("gate", "up", "down")]

        def bank(name, b=0, k=0):
            return misc[:, JOBS.index((name, b, k)) % 2, :]

        PIECES = 17
        PIECE_LOADS = [16] * 6 + [32] * 6 + [16] * 5

        def piece_loaded(n):
            return sum(PIECE_LOADS[m] for m in range(n % 3, n + 1, 3))

        def piece_at(n):
            if n < 12:
                hi, lo = ((upA_hi, upA_lo), (upC_hi, upC_lo))[n // 6]
                k = n % 6
                at = {0: 0, 1: STG, 2: 4 * STG, 3: 2 * STG, 4: 3 * STG, 5: 5 * STG}[k]
                return hi[:, at:at + STG], lo[:, at:at + STG], STG
            tiles = 4 if n < 16 else 2
            t = 4 * (n - 12)
            return down[:, t:t + tiles, 0:D], down[:, t:t + tiles, D:2 * D], tiles * D

        def gate_col(t):
            return P * t if t < RT else 4 * STG + P * (t - RT)

        def up_col(t):
            return 2 * STG + P * t if t < RT else 5 * STG + P * (t - RT)

        @block.sync
        def _(sp):
            def load_chunk(q, c):
                tile, j = divmod(c, G // 2)
                for k in range(2):
                    row = PATCH * (2 * j + k)
                    sp.dma_start(ring[:, c % RING, HW * k:HW * (k + 1)],
                                 x_rows[bass.ds(2 * C * q + 8 * tile, 8), row:row + PATCH, :]).then_inc(s_chunk[c % RING], 16)

            def load_text(q, b):
                src = txt[bass.ds(2 * q + b, 1), :, :].rearrange("b t d -> (b t) d")
                cut = 2 * TM - IMG
                sp.dma_start(h[IMG - TM:TM, b, 1, :], src[0:cut, :]).then_inc(s_txt[b], 16)
                sp.dma_start(h[0:TM, b, 2, :], src[cut:cut + TM, :]).then_inc(s_txt[b], 16)

            def store(beta):
                wait(sp, s_res, beta + 1)
                dst = out[bass.ds(beta, 1), :, :].rearrange("b (m p) d -> p (b m) d", p=TM)
                sp.dma_start(dst, res[0:TM, :, :]).then_inc(s_out, 16)

            def spread_gates(beta, b):
                if isinstance(beta, int) and beta == 0:
                    sp.wait_ge(s_stage_lo, PIECES)
                    sp.wait_ge(s_prep_w, 1)
                wait(sp, s_gs, beta + 1)
                wait(sp, s_gated, T * (beta - 1) + RT)
                sp.dma_start(routed_gates_dram[0:NE + 1, :], gs[:, :]).then_inc(s_gdram, 16)
                wait(sp, s_gdram, 16 * (beta + 1))
                sp.dma_start(gate_bc[:, :, :].rearrange("p e l -> p (e l)"),
                             routed_gates_dram[0:NE, :].rearrange("(o e) l -> o (e l)", o=1).broadcast_to([P, NE * L])
                             ).then_inc(s_gbc, 16)
                sp.dma_start(alpha_bc[:, b, :], routed_gates_dram[NE:NE + 1, :].broadcast_to([P, L])).then_inc(s_gbc, 16)

            def iteration(i, mlp, carry, mix, pooling):
                more = pooling and (not isinstance(i, int) or i <= NP - 4)
                for name, b, c in steps(SP_STEPS, 0):
                    if name == "store" and b == 1 and carry:
                        store(2 * i - 1)
                    elif name == "store" and b == 0 and mlp:
                        store(2 * i)
                    elif name == "gates" and b == 1 and mlp:
                        spread_gates(2 * i + 1, 1)
                    elif name == "gates" and b == 0 and mix:
                        spread_gates(2 * i + 2, 0)
                    elif name == "text" and b == 1 and mix:
                        wait(sp, s_hf, 2 * (2 * i + 1) + 2 if mlp else 0)
                        load_text(i + 1, 1)
                    elif name == "text" and b == 0 and pooling:
                        if mix:
                            wait(sp, s_hf, 2 * (2 * i + 2) + 2)
                        load_text(i + 2, 0)
                    elif name == "load" and (pooling if c + RING < CHUNKS else more):
                        wait(sp, s_pooled, CHUNKS * (i + 2) + c + 1)
                        load_chunk(*((i + 2, c + RING) if c + RING < CHUNKS else (i + 3, c + RING - CHUNKS)))

            for c in range(RING):
                load_chunk(0, c)
            pieces = []
            for part in range(2):
                for w, ws in ((w_gate, ws_gate), (w_up, ws_up)):
                    rows = slice(0, P) if part == 0 else slice(P, D)
                    pieces += [(part, w[0:4, rows, :].rearrange("e d n -> d e n")), (part, w[4:8, rows, :].rearrange("e d n -> d e n")),
                               (part, ws[rows, :])]
            wd = w_down.rearrange("e n d -> (e n) d")
            pieces += [(2, wd[4 * P * k:4 * P * (k + 1), :].rearrange("(t p) d -> p t d", p=P)) for k in range(3)]
            pieces += [(2, ws_down[0:4 * P, :].rearrange("(t p) d -> p t d", p=P)),
                       (2, ws_down[4 * P:6 * P, :].rearrange("(t p) d -> p t d", p=P))]
            for n, (part, src) in enumerate(pieces):
                wait(sp, s_stage_lo, n - 2)
                dst = stage[n % 3]
                if len(src.shape) == 3:
                    dst = dst[:, 0:src.shape[1] * D].rearrange("p (e n) -> p e n", n=D)
                if part == 1:
                    sp.dma_start(dst[0:R], src).then_inc(s_stage[n % 3], 16)
                    sp.dma_start(dst[R:P], src).then_inc(s_stage[n % 3], 16)
                else:
                    sp.dma_start(dst, src).then_inc(s_stage[n % 3], 16)
            iterations(sp, iteration, NP - 4)
            store(2 * NP - 1)
            wait(sp, s_out, 16 * 2 * NP)

        @block.gpsimd
        def _(pool):
            pool.memset(chan[:, :, :], 0.0).then_inc(s_zeroed, 1)
            pool.memset(woutf_st[:, :, :], 0.0).then_inc(s_zeroed, 1)
            pool.memset(bout_st, 0.0).then_inc(s_zeroed, 1)
            pool.memset(rt_st[:, :, :], 0.0).then_inc(s_zeroed, 1)
            pool.memset(ident[:, :], 0.0).then_inc(s_const_chain, 1)
            pool.wait_ge(s_const_chain, 1)
            pool.affine_select(out=ident[:, :], in_=ident[:, :], compare_op=ALU.not_equal, fill=1.0, base=0,
                               pattern=[[-1, P]], channel_multiplier=1).then_inc(s_const, 1)
            pool.memset(col[:, MHI:MHI + 1], 1.0).then_inc(s_const_chain, 1)
            pool.memset(col[:, MLO:MLO + 1], 1.0).then_inc(s_const_chain, 1)
            pool.wait_ge(s_const_chain, 3)
            pool.affine_select(out=col[:, MHI:MHI + 1], in_=col[:, MHI:MHI + 1], compare_op=ALU.is_ge, fill=0.0,
                               base=63, pattern=[[0, 1]], channel_multiplier=-1).then_inc(s_const_chain, 1)
            pool.affine_select(out=col[:, MLO:MLO + 1], in_=col[:, MLO:MLO + 1], compare_op=ALU.is_ge, fill=0.0,
                               base=-64, pattern=[[0, 1]], channel_multiplier=1).then_inc(s_const_chain, 1)
            pool.wait_ge(s_const_chain, 5)
            pool.affine_select(out=col[:, MHI:MHI + 1], in_=col[:, MHI:MHI + 1], compare_op=ALU.not_equal, fill=1.0,
                               base=-96, pattern=[[0, 1]], channel_multiplier=1).then_inc(s_const, 1)
            pool.affine_select(out=col[:, MLO:MLO + 1], in_=col[:, MLO:MLO + 1], compare_op=ALU.not_equal, fill=0.0,
                               base=-96, pattern=[[0, 1]], channel_multiplier=1).then_inc(s_const, 1)
            pool.iota(iota_i[:, :], pattern=[[-1, L]], base=L - 1, channel_multiplier=0).then_inc(s_const_chain, 1)
            pool.wait_ge(s_const_chain, 6)
            pool.tensor_copy(khalf[:, :], iota_i[0:32, :]).then_inc(s_const_chain, 1)
            pool.tensor_copy(biota[:, :], iota_i[:, L - NE:L]).then_inc(s_const_chain, 1)
            pool.wait_ge(s_const_chain, 8)
            pool.tensor_scalar(khalf[:, :], khalf[:, :], 0.5, None, ALU.mult).then_inc(s_const, 1)
            pool.tensor_scalar(biota[:, :], biota[:, :], -1.0, float(NE - 1), ALU.mult, ALU.add).then_inc(s_const, 1)
            pool.memset(power[:, :], -0.5).then_inc(s_const, 1)
            pool.memset(xin[:, :, 0:3], 0.0).then_inc(s_const, 1)

            def gate_step(i, s):
                n, b, t = SLOTS * i + s, s // T, s % T
                wait(pool, s_sil, n + 1)
                buf = hid[:, s % 3, :]
                if t == 0:
                    wait(pool, s_gbc, 32 * (2 * i + b + 1))
                if t < RT:
                    lo_e, hi_e = (P * t) // D, (P * t + P - 1) // D
                    if lo_e == hi_e:
                        pool.tensor_tensor(buf, buf, gate_bc[:, lo_e, :], ALU.mult).then_inc(s_gated, 1)
                    else:
                        pool.tensor_tensor(hid[0:64, s % 3, :], hid[0:64, s % 3, :], gate_bc[0:64, lo_e, :], ALU.mult)
                        wait(pool, s_gated, n)
                        pool.tensor_tensor(hid[64:P, s % 3, :], hid[64:P, s % 3, :], gate_bc[64:P, hi_e, :],
                                           ALU.mult).then_inc(s_gated, 1)
                        wait(pool, s_gated, n + 1)
                else:
                    pool.tensor_tensor(buf, buf, alpha_bc[:, b, :], ALU.mult).then_inc(s_gated, 1)

            def rstd_of(beta, k, ready, done):
                wait(pool, ready, beta + 1)
                pool.tensor_tensor(rstd[0:TM, k, :], rstd[0:TM, k, :], power[0:TM, :], ALU.pow).then_inc(done, 1)

            def add_y(beta, b, k):
                wait(pool, s_yz, 2 * beta + k + 1)
                m = slice(0, 2) if k == 0 else slice(2, 3)
                pool.tensor_tensor(h[0:TM, b, m, :], h[0:TM, b, m, :], yz[0:TM, m, 0:D], ALU.add).then_inc(s_hy, 1)
                pool.tensor_copy(
                    zs[0:TM, m, :].rearrange("p m (k b n) -> p m k b n", k=2, b=2)[:, :, :, b, :],
                    yz[0:TM, m, D:NX].rearrange("p m (k n) -> p m k n", k=2)).then_inc(s_zs, 1)

            def iteration(i, mlp, carry, mix, pooling):
                for s in range(SLOTS):
                    for name, b, k in steps(POOL_STEPS, s):
                        if name == "gated":
                            if mlp:
                                gate_step(i, s)
                            continue
                        q = pair_of(i, name, b, mlp, mix)
                        if q is None:
                            continue
                        beta = 2 * q + b
                        if name == "rstd":
                            rstd_of(beta, b, s_rstd_a, s_rstd)
                        elif name == "rstdf":
                            rstd_of(beta, 2 + b, s_rstdf_a, s_rstdf)
                        elif name == "addy":
                            add_y(beta, b, k)
                        elif name == "scanin":
                            wait(pool, s_exp2, q + 1)
                            pool.tensor_tensor(sc[5], sc[0], sc[0], ALU.mult).then_inc(s_ab, 1)
                            wait(pool, s_dsev, q + 1)
                            pool.tensor_tensor(sc[2], sc[2], sc[0], ALU.mult).then_inc(s_ab, 1)
                        else:
                            raise AssertionError(name)

            iterations(pool, iteration, FULL)

        @block.scalar
        def _(act):
            loads = []

            def load(dst, src):
                act.dma_start(dst, src, allow_slow_non_contiguous=True).then_inc(s_small, 16)
                loads.append(1)

            def column(ap):
                return ap.rearrange("(p o) -> p o", o=1)

            load(col[:, GA:GA + 1], column(ln_g[0:P]))
            load(col[0:R, GC:GC + 1], column(ln_g[P:D]))
            load(col[R:P, GC:GC + 1], column(ln_g[P:D]))
            load(lnb[:, 0:1], column(ln_b[0:P]))
            load(lnb[0:R, 1:2], column(ln_b[P:D]))
            load(col[:, BIN:BIN + KE], b_in.rearrange("(k p) -> p k", p=P))
            load(col[:, BCV:BCV + KE], b_conv.rearrange("(k p) -> p k", p=P))
            for b in range(2):
                load(col[NST * b:NST * (b + 1), BDT:BDT + 1], column(b_dt))
                load(col[NST * b:NST * (b + 1), BDS:BDS + 1], column(b_xp[D:D + NST]))
            load(col[:, SGB:SGB + 1], sg_b.rearrange("(p o) -> p o", o=1).broadcast_to([P, 1]))
            load(col[:, USC:USC + 1], column(b_us[0:P]))
            load(col[0:R, USC + 1:USC + 2], column(b_us[P:D]))
            load(col[:, XPC:XPC + 1], column(b_xp[0:P]))
            load(col[0:R, XPC + 1:XPC + 2], column(b_xp[P:D]))
            load(taps[:, :, :], W_conv.rearrange("(k p) o t -> p k (o t)", p=P))
            load(win_st[0], W_in[0:P, :])
            load(win_st[1][0:R], W_in[P:D, :])
            load(win_st[1][R:P], W_in[P:D, :])
            load(wxp_st, W_xp.rearrange("(k p) n -> p k n", p=P))
            load(wdt_st, W_dt.rearrange("(k p) n -> p k n", p=P))
            load(wout_st[0], W_out[0:P, :])
            load(wout_st[1], W_out[P:D, :])
            load(wus_st, W_us)
            act.wait_ge(s_zeroed, 4)
            load(woutf_st[R:P, 1, :], W_out[D:2 * P, :])
            load(woutf_st[:, 2, :], W_out[2 * P:3 * P, :])
            load(bout_st[96:97, :], b_out.rearrange("(o d) -> o d", o=1))
            load(bout_st[97:98, :], b_out.rearrange("(o d) -> o d", o=1))
            load(rt_st[:, 0, 0:NE], router_w[0:P, :])
            load(rt_st[:, 0, NE:NE + 1], sg_w[0:P, :])
            for half in range(2):
                load(rt_st[R * half:R * (half + 1), 1, 0:NE], router_w[P:D, :])
                load(rt_st[R * half:R * (half + 1), 1, NE:NE + 1], sg_w[P:D, :])
            for k, (first, rows) in enumerate(((0, range(8)), (8, range(4)), (0, range(4, 8)), (4, range(8)))):
                for n, r in enumerate(rows):
                    load(chan[PATCH * r:PATCH * (r + 1), k, :], cw[first + n:first + n + 1, :].broadcast_to([PATCH, D]))
            assert len(loads) == SMALL_COUNT, len(loads)

            for f in range(KE):
                act.wait_ge(s_prep_pe, f + 1)
                act.activation(wxpT[0][:, P * f:P * (f + 1)], gu[:, f, 0:P], ACT.Copy)
                act.activation(wxpT[1][:, P * f:P * (f + 1)], gu[0:R, f, P:2 * P], ACT.Copy).then_inc(s_prep_act, 1)
            for n in range(PIECES):
                act.wait_ge(s_stage[n % 3], piece_loaded(n))
                hi, _, w = piece_at(n)
                src = stage[n % 3][:, 0:w]
                if n >= 12:
                    src = src.rearrange("p (t d) -> p t d", d=D)
                act.activation(hi, src, ACT.Copy).then_inc(s_stage_hi, 1)
            act.wait_ge(s_const, 7)
            act.wait_ge(s_small, 16 * SMALL_COUNT)
            act.wait_ge(s_prep_w, 1)

            def evac_pool(beta, b):
                wait(act, s_job["pool"], beta + 1)
                wait(act, s_hf, 2 * beta - 2)
                act.activation(h[0:TM, b, 0, :], bank("pool", b)[0:TM, 0:D], ACT.Copy)
                act.activation(h[0:IMG - TM, b, 1, :], bank("pool", b)[0:IMG - TM, D:2 * D], ACT.Copy).then_inc(s_tokens, 1)

            def double_tail(beta, norm, done, dst):
                wait(act, norm, beta + 1)
                act.activation(dst[0:TM, :, D:2 * P], dst[0:TM, :, P:D], ACT.Copy).then_inc(done, 1)

            def evac_hi(beta, b, name, dst, done):
                wait(act, s_job[name], beta + 1)
                act.activation(dst, bank(name, b)[:, 0:L], ACT.Copy).then_inc(done, 1)

            def evac_in(beta, b, e):
                k = 3 * beta + e
                wait(act, s_job["in"], k + 1)
                wait(act, s_actlo, k - 2)
                act.activation(xin[:, e, 3:3 + L], bank("in", b, e)[:, 0:L], ACT.Identity,
                               bias=binf[:, e:e + 1])
                act.activation(conv[:, e, :], bank("in", b, e)[:, 0:L], ACT.Identity, bias=bconv[:, e:e + 1],
                               scale=taps[:, e, 3:4]).then_inc(s_xin, 1)

            def silu_mix(beta, e):
                k = 3 * beta + e
                wait(act, s_tap, 3 * (k + 1))
                act.activation(xin[:, e, 3:3 + L], conv[:, e, :], ACT.Silu).then_inc(s_silu1, 1)
                if e == 0:
                    wait(act, s_job["act"], 2 * beta)
                act.activation(act_hi[:, e, :], conv[:, e, :], ACT.Silu).then_inc(s_acthi, 1)

            def evac_act(beta, b, k):
                wait(act, s_job["act"], 2 * beta + k + 1)
                if k == 0:
                    wait(act, s_zs, 2 * beta)
                    act.activation(yz[0:TM, 0:2, :], bank("act", b, 0)[0:TM, 0:2 * NX].rearrange("p (m n) -> p m n", m=2),
                                   ACT.Copy).then_inc(s_yz, 1)
                else:
                    act.activation(yz[0:TM, 2, :], bank("act", b, 1)[0:TM, 0:NX], ACT.Copy).then_inc(s_yz, 1)

            def scan_dt(q):
                wait(act, s_job["dt"], q + 1)
                act.activation(sc[0], bank("dt")[0:32, 0:L], ACT.Abs, bias=col[0:32, BDT:BDT + 1]).then_inc(s_exp1, 1)
                act.activation(sc[1], bank("dt")[0:32, 0:L], ACT.Relu, bias=col[0:32, BDT:BDT + 1]).then_inc(s_dtev, 1)

            def scan_ds(q):
                wait(act, s_job["ds"], q + 1)
                act.activation(sc[2], bank("ds")[0:32, 0:L], ACT.Identity, bias=col[0:32, BDS:BDS + 1]).then_inc(s_dsev, 1)

            def scan_exp(q):
                act.preload_act_table_set("natural_log_exp_and_others")
                wait(act, s_exp1, 2 * q + 1)
                act.activation(sc[0], sc[0], ACT.Exp, scale=-1.0).then_inc(s_exp1, 1)

            def scan_ln(q):
                wait(act, s_scan_w, q + 1)
                act.activation(sc[4], sc[3], ACT.Ln).then_inc(s_ln, 1)

            def scan_exp_half(q):
                wait(act, s_dtdone, q + 1)
                act.activation(sc[0], sc[4], ACT.Exp, scale=-0.5).then_inc(s_exp2, 1)

            def scan_tanh(q):
                wait(act, s_dtdone, q + 1)
                act.activation(sc[1], sc[4], ACT.Tanh, scale=0.5).then_inc(s_tanh1, 1)
                wait(act, s_kd, q + 1)
                act.activation(sc[3], sc[3], ACT.Tanh).then_inc(s_tanhk, 1)

            def us_hi(q):
                wait(act, s_usf, q + 1)
                act.activation(us[0:32, :], sc[1], ACT.Copy).then_inc(s_ushi, 1)
                act.activation(us[64:96, :], sc[1], ACT.Copy).then_inc(s_ushi, 1)

            def gate_tanh(beta):
                wait(act, s_diff, beta + 1)
                act.activation(gsc[0:TM, 1, :], gsc[0:TM, 0, :], ACT.Tanh, scale=-0.5)
                act.activation(gsc[0:TM, 2, :], logit[0:TM, :, NE], ACT.Tanh, scale=0.5,
                               bias=sgbh[0:TM, :]).then_inc(s_gtanh, 1)

            def evac_gates(beta, b):
                wait(act, s_job["gates"], beta + 1)
                wait(act, s_gdram, 16 * beta)
                act.activation(gs[:, :], bank("gates", b)[0:NE + 1, 0:L], ACT.Copy).then_inc(s_gs, 1)

            def hidden_hi(i, s):
                n = SLOTS * i + s
                wait(act, s_hid, n + 1)
                wait(act, s_down, n - 2)
                act.activation(hid_hi[:, s % 3, :], hid[:, s % 3, :], ACT.Copy).then_inc(s_hi, 1)

            def silu_step(i, s):
                n = SLOTS * i + s
                wait(act, s_g, n + 1)
                wait(act, s_lo, n - 2)
                act.activation(hid[:, s % 3, :], gu[:, 0, 0:L], ACT.Silu).then_inc(s_sil, 1)

            def step(name, b, k, q):
                beta = 2 * q + b
                if name == "pool":
                    evac_pool(beta, b)
                elif name == "double":
                    double_tail(beta, s_norm, s_dup, xn)
                elif name == "doublef":
                    double_tail(beta, s_normf, s_dupf, xnf)
                elif name == "mixA":
                    wait(act, s_job["in"], 3 * beta)
                    evac_hi(beta, b, "mixA", mixA_hi[:, :], s_mixhi)
                elif name == "mixC":
                    evac_hi(beta, b, "mixC", mixC[:, :], s_mixc0)
                elif name == "in":
                    evac_in(beta, b, k)
                elif name == "convsilu":
                    silu_mix(beta, k)
                elif name == "act":
                    evac_act(beta, b, k)
                elif name == "dt":
                    scan_dt(q)
                elif name == "ds":
                    scan_ds(q)
                elif name == "exp":
                    scan_exp(q)
                elif name == "ln":
                    scan_ln(q)
                elif name == "exp2":
                    scan_exp_half(q)
                elif name == "tanh":
                    scan_tanh(q)
                elif name == "states":
                    us_hi(q)
                elif name == "mlpA":
                    wait(act, s_u, T * (beta - 1))
                    evac_hi(beta, b, "mlpA", mlpA_hi[:, b, :], s_mlphi)
                elif name == "mlpC":
                    evac_hi(beta, b, "mlpC", mlpC[:, b, :], s_mlpc0)
                elif name == "gtanh":
                    gate_tanh(beta)
                elif name == "gates":
                    evac_gates(beta, b)
                else:
                    raise AssertionError(name)

            def iteration(i, mlp, carry, mix, pooling):
                for s in range(SLOTS):
                    for name, b, k in steps(ACT_STEPS, s):
                        if name == "silu":
                            if mlp:
                                silu_step(i, s)
                        elif name == "hi":
                            if mlp and s > 0:
                                hidden_hi(i, s - 1)
                            elif carry:
                                hidden_hi(i - 1, SLOTS - 1)
                        elif pair_of(i, name, b, mlp, mix) is not None:
                            step(name, b, k, pair_of(i, name, b, mlp, mix))

            iterations(act, iteration, FULL)
            hidden_hi(NP - 1, SLOTS - 1)

        @block.vector
        def _(dve):
            chained = [0]

            def chain(ins):
                chained[0] += 1
                ins.then_inc(s_prep_dve, 1)
                dve.wait_ge(s_prep_dve, chained[0])

            dve.wait_ge(s_small, 16 * SMALL_COUNT)
            dve.wait_ge(s_const, 7)
            chain(dve.memset(us[96:128, :].bitcast(F32), 1.0))
            dve.wait_ge(s_prep_pe, 4)
            chain(dve.tensor_tensor(binf[:, :], prep[:, 0:KE], col[:, BIN:BIN + KE], ALU.add))
            chain(dve.tensor_tensor(bconv[:, :], binf[:, :], taps[:, :, 3], ALU.mult))
            chain(dve.tensor_tensor(bconv[:, :], bconv[:, :], col[:, BCV:BCV + KE], ALU.add))
            chain(dve.tensor_scalar(sgbh[:, :], col[:, SGB:SGB + 1], 0.5, None, ALU.mult))
            for st, g, hi, lo in ((win_st[0], GA, inA_hi, inA_lo), (win_st[1], GC, inC_hi, inC_lo)):
                chain(dve.tensor_scalar(st, st, col[:, g:g + 1], None, ALU.mult))
                chain(dve.tensor_copy(hi[:, :], st))
                chain(dve.tensor_tensor(lo[:, :], st, hi[:, :].bitcast(F32), ALU.subtract))
            for f in range(KE):
                dve.wait_ge(s_prep_pe, 5 + f)
                full = wx_full[:, f, :]
                chain(dve.tensor_tensor(full[:, 0:D], gu[:, f, 0:D], woutf_st[:, f, :], ALU.add))
                chain(dve.tensor_copy(full[:, D:D + NST], wdt_st[:, f, :]))
                chain(dve.tensor_copy(full[:, D + NST:NX], wxp_st[:, f, D:D + NST]))
                chain(dve.tensor_copy(actw_hi[:, f, :], full))
                chain(dve.tensor_tensor(actw_lo[:, f, :], full, actw_hi[:, f, :].bitcast(F32), ALU.subtract))
            dve.wait_ge(s_prep_pe, 8)
            for part, rows in ((0, P), (1, R)):
                chain(dve.memset(uslT[part][:, :, :], 0.0))
                for b in range(2):
                    for q in range(3):
                        at = 32 * q + NST * b
                        chain(dve.tensor_copy(uslT[part][:, b, at:at + NST], prep[0:rows, NST * part:NST * (part + 1)]))
                    for c in (96, 97):
                        ins = dve.tensor_tensor(uslT[part][:, b, c:c + 1], col[0:rows, USC + part:USC + part + 1],
                                                col[0:rows, XPC + part:XPC + part + 1], ALU.add)
            ins.then_inc(s_usl, 1)
            for b in range(2):
                dve.wait_ge(s_prep_pe, 9 + b)
                chain(dve.tensor_tensor(uw, acc[:, b, 0:D], bout_st, ALU.add))
                chain(dve.tensor_copy(usw[:, b, :], uw))
                chain(dve.tensor_tensor(uw, uw, usw[:, b, :].bitcast(F32), ALU.subtract))
                chain(dve.tensor_scalar(uw, uw, col[:, MLO:MLO + 1], None, ALU.mult))
                chain(dve.scalar_tensor_tensor(usw[:, b, :], usw[:, b, :].bitcast(F32), col[:, MHI:MHI + 1], uw,
                                               ALU.mult, ALU.add))
            for part, w in ((0, routeA), (1, routeC)):
                chain(dve.tensor_copy(w[:, 0:16], rt_st[:, part, :]))
                ins = dve.tensor_tensor(w[:, 16:32], rt_st[:, part, :], w[:, 0:16].bitcast(F32), ALU.subtract)
            ins.then_inc(s_prep_w, 1)

            for n in range(PIECES):
                dve.wait_ge(s_stage_hi, n + 1)
                hi, lo, w = piece_at(n)
                src = stage[n % 3][:, 0:w]
                if n >= 12:
                    src = src.rearrange("p (t d) -> p t d", d=D)
                dve.tensor_tensor(lo, src, hi.bitcast(F32), ALU.subtract).then_inc(s_stage_lo, 1)

            def pool_chunk(q, c):
                tile, j = divmod(c, G // 2)
                wait(dve, s_chunk[c % RING], 32 * (3 * q + tile + 1))
                if j == 0:
                    wait(dve, s_job["pool"], 2 * q)
                dve.tensor_reduce(pooled[:, tile, 2 * G * j:2 * G * (j + 1)],
                                  ring[:, c % RING, :].rearrange("p (t k) -> p t k", k=PATCH), AX_X,
                                  ALU.add).then_inc(s_pooled, 1)

            def settle(s, value):
                wait(dve, s, value)
                dve.memset(settled[:, :], 0.0)

            def stats_of(beta, b, k, src, chain_sem, aggregated, done, slope, offset):
                for m in range(3):
                    ins = dve.bn_stats(stats[0:TM, k, m, :], src[0:TM, b, m, :])
                ins.then_inc(chain_sem, 1)
                settle(chain_sem, beta + 1)
                for m in range(3):
                    ins = dve.bn_aggr(mv[0:TM, k, m, :], stats[0:TM, k, m, :])
                ins.then_inc(aggregated, 1)
                wait(dve, aggregated, beta + 1)
                dve.tensor_scalar(rstd[0:TM, k, :], mv[0:TM, k, :, 1], slope, offset, ALU.mult, ALU.add).then_inc(done, 1)

            def normalise(beta, b, k, src, dst, ready, done, own):
                wait(dve, ready, beta + 1)
                wait(dve, own, beta + 1)
                for m in range(3):
                    ins = dve.tensor_scalar(dst[0:TM, m, 0:D], src[0:TM, b, m, :], mv[0:TM, k, m, 0:1],
                                            rstd[0:TM, k, m:m + 1], ALU.subtract, ALU.mult)
                ins.then_inc(done, 1)

            def split_A(beta, src, hi_ready, hi, lo, done):
                wait(dve, hi_ready, beta + 1)
                dve.tensor_tensor(lo, src[:, 0:L], hi.bitcast(F32), ALU.subtract).then_inc(done, 1)

            def split_C(beta, src, hi_ready, both, done):
                wait(dve, hi_ready, beta + 1)
                dve.tensor_tensor(both[64:P], src[64:P, 0:L], both[64:P].bitcast(F32), ALU.subtract).then_inc(done, 1)

            def conv_taps(beta, e):
                k = 3 * beta + e
                wait(dve, s_xin, k + 1)
                for j in range(3):
                    if j:
                        wait(dve, s_tap, 3 * k + j)
                    dve.scalar_tensor_tensor(conv[:, e, :], xin[:, e, 2 - j:2 - j + L], taps[:, e, 2 - j:3 - j],
                                             conv[:, e, :], ALU.mult, ALU.add).then_inc(s_tap, 1)

            def act_lo_of(beta, e):
                wait(dve, s_acthi, 3 * beta + e + 1)
                dve.tensor_tensor(act_lo[:, e, :], xin[:, e, 3:3 + L], act_hi[:, e, :].bitcast(F32),
                                  ALU.subtract).then_inc(s_actlo, 1)

            def scan_1(q, part):
                base = 13 * q
                if part == 0:
                    wait(dve, s_exp1, 2 * q + 2)
                    dve.tensor_scalar(sc[3], sc[0], 1.0, None, ALU.add).then_inc(s_scan_w, 1)
                    wait(dve, s_scan_w, q + 1)
                    dve.scalar_tensor_tensor(sc[5], sc[3], -1.0, sc[0], ALU.add, ALU.subtract).then_inc(s_scan, 1)
                    wait(dve, s_scan, base + 1)
                    return
                wait(dve, s_ln, q + 1)
                dve.tensor_tensor(sc[4], sc[4], sc[5], ALU.subtract).then_inc(s_scan, 1)
                wait(dve, s_scan, base + 2)
                dve.scalar_tensor_tensor(sc[4], sc[0], 0.69, sc[4], ALU.mult, ALU.max).then_inc(s_scan, 1)
                wait(dve, s_scan, base + 3)
                wait(dve, s_dtev, q + 1)
                dve.tensor_tensor(sc[4], sc[4], sc[1], ALU.add).then_inc(s_dtdone, 1)
                wait(dve, s_dtdone, q + 1)
                dve.tensor_tensor(sc[3], sc[4], khalf[:, :], ALU.mult).then_inc(s_kd, 1)

            def scan_2(q, part):
                base = 13 * q + 3
                if part == 0:
                    wait(dve, s_ab, 2 * q + 2)
                    dve.tensor_tensor_scan(sc[6], sc[5], sc[2], 0.0, ALU.mult, ALU.add).then_inc(s_scan, 1)
                    wait(dve, s_tanh1, q + 1)
                    wait(dve, s_tanhk, q + 1)
                    dve.tensor_scalar(sc[4], sc[1], 2.0, 1e-30, ALU.mult, ALU.max).then_inc(s_scan, 1)
                    wait(dve, s_scan, base + 2)
                    dve.scalar_tensor_tensor(sc[0], sc[3], 1.0, sc[4], ALU.add, ALU.mult).then_inc(s_scan, 1)
                    dve.scalar_tensor_tensor(sc[1], sc[1], 1.0, sc[2], ALU.add, ALU.mult).then_inc(s_scan, 1)
                elif part == 1:
                    wait(dve, s_scan, base + 3)
                    dve.reciprocal(sc[0], sc[0]).then_inc(s_scan, 1)
                elif part == 2:
                    wait(dve, s_scan, base + 4)
                    dve.scalar_tensor_tensor(sc[1], sc[3], 2.0, sc[1], ALU.mult, ALU.mult).then_inc(s_scan, 1)
                    wait(dve, s_scan, base + 5)
                    dve.tensor_tensor(sc[4], sc[4], sc[0], ALU.mult).then_inc(s_scan, 1)
                    wait(dve, s_scan, base + 6)
                    dve.tensor_tensor(sc[1], sc[1], sc[0], ALU.mult).then_inc(s_scan, 1)
                    wait(dve, s_scan, base + 7)
                    dve.scalar_tensor_tensor(sc[3], sc[3], -1.0, sc[4], ALU.add, ALU.mult).then_inc(s_scan, 1)
                else:
                    wait(dve, s_scan, base + 9)
                    dve.tensor_tensor(sc[3], sc[3], sc[6], ALU.mult).then_inc(s_scan, 1)
                    wait(dve, s_scan, base + 10)
                    dve.tensor_tensor(sc[1], sc[1], sc[3], ALU.subtract).then_inc(s_usf, 1)

            def us_lo(q):
                wait(dve, s_ushi, 2 * q + 1)
                dve.tensor_tensor(us[32:64, :], sc[1], us[0:32, :].bitcast(F32), ALU.subtract).then_inc(s_uslo, 1)

            def evac_us(beta, b, k):
                wait(dve, s_job["us"], 2 * beta + k + 1)
                wait(dve, s_hy, 2 * beta + k + 1)
                m = slice(0, 2) if k == 0 else slice(2, 3)
                n = 2 if k == 0 else 1
                dve.tensor_tensor(hf[0:TM, b, m, :], bank("us", b, k)[0:TM, 0:n * D].rearrange("p (m d) -> p m d", m=n),
                                  h[0:TM, b, m, :], ALU.add).then_inc(s_hf, 1)

            def evac_route(beta, b):
                wait(dve, s_job["route"], beta + 1)
                dve.tensor_copy(lg[0:TM, :, :], bank("route", b)[0:TM, 0:96].rearrange("p (m n) -> p m n", m=3)).then_inc(s_lg, 1)

            GCH = 8

            def gates_1(beta):
                base = GCH * beta
                wait(dve, s_lg, beta + 1)
                dve.tensor_tensor(logit[0:TM, :, :], lg[0:TM, :, 0:16], lg[0:TM, :, 16:32], ALU.add).then_inc(s_gate, 1)
                settle(s_gate, base + 1)
                for m in range(3):
                    ins = dve.max(top[0:TM, m, :], logit[0:TM, m, 0:NE])
                ins.then_inc(s_gate, 1)
                wait(dve, s_gate, base + 2)
                dve.tensor_tensor(gsc[0:TM, 0, :], top[0:TM, :, 1], top[0:TM, :, 0], ALU.subtract).then_inc(s_diff, 1)
                for m in range(3):
                    ins = dve.max_index(topi[0:TM, m, :], top[0:TM, m, :], logit[0:TM, m, 0:NE])
                ins.then_inc(s_gate, 1)
                wait(dve, s_gate, base + 3)
                dve.tensor_copy(topf[0:TM, :, :], topi[0:TM, :, :]).then_inc(s_gate, 1)
                wait(dve, s_gate, base + 4)
                for r in range(2):
                    ins = dve.tensor_tensor(pick[0:TM, r, :, :],
                                            biota[0:TM, :].unsqueeze(1).broadcast_to([TM, 3, NE]),
                                            topf[0:TM, :, r:r + 1].broadcast_to([TM, 3, NE]), ALU.is_equal)
                ins.then_inc(s_gate, 1)

            def gates_2(beta):
                base = GCH * beta + 5
                wait(dve, s_gtanh, beta + 1)
                g = gsc[0:TM, :, :]
                dve.tensor_scalar(g[:, 3, :], g[:, 1, :], 0.5, 0.5, ALU.mult, ALU.add)
                dve.tensor_scalar(g[:, 4, :], g[:, 1, :], -0.5, 0.5, ALU.mult, ALU.add)
                dve.tensor_scalar(g[:, 5, :], g[:, 2, :], -0.5, 0.5, ALU.mult, ALU.add)
                dve.tensor_scalar(gt[0:TM, :, NE], g[:, 2, :], 0.5, 0.5, ALU.mult, ALU.add).then_inc(s_gate, 1)
                wait(dve, s_gate, base + 1)
                dve.tensor_tensor(g[:, 6, :], g[:, 3, :], g[:, 5, :], ALU.mult)
                dve.tensor_tensor(g[:, 7, :], g[:, 4, :], g[:, 5, :], ALU.mult).then_inc(s_gate, 1)
                wait(dve, s_gate, base + 2)
                for r in range(2):
                    ins = dve.tensor_tensor(pick[0:TM, r, :, :], pick[0:TM, r, :, :],
                                            g[:, 6 + r, :].unsqueeze(2).broadcast_to([TM, 3, NE]), ALU.mult)
                ins.then_inc(s_gate, 1)
                wait(dve, s_gate, base + 3)
                dve.tensor_tensor(gt[0:TM, :, 0:NE], pick[0:TM, 0, :, :], pick[0:TM, 1, :, :], ALU.add).then_inc(s_gt, 1)

            def hidden(i, s):
                n = SLOTS * i + s
                wait(dve, s_u, n + 1)
                wait(dve, s_gated, n + 1)
                dve.tensor_tensor(hid[:, s % 3, :], gu[:, 1 + s % 2, 0:L], hid[:, s % 3, :], ALU.mult).then_inc(s_hid, 1)

            def hidden_lo(i, s):
                n = SLOTS * i + s
                wait(dve, s_hi, n + 1)
                wait(dve, s_down, n - 2)
                dve.tensor_tensor(hid_lo[:, s % 3, :], hid[:, s % 3, :], hid_hi[:, s % 3, :].bitcast(F32),
                                  ALU.subtract).then_inc(s_lo, 1)

            def result(beta, b):
                wait(dve, s_down, T * (beta + 1))
                wait(dve, s_out, 16 * beta)
                dve.tensor_tensor(res[0:TM, :, :], acc[0:TM, :, 0:D], hf[0:TM, b, :, :], ALU.add).then_inc(s_res1, 1)
                wait(dve, s_res1, beta + 1)
                dve.tensor_tensor(res[0:TM, :, :], acc[0:TM, :, D:2 * D], res[0:TM, :, :], ALU.add).then_inc(s_res, 1)

            def step(name, b, k, q):
                beta = 2 * q + b
                if name == "stats":
                    wait(dve, s_tokens, beta + 1)
                    wait(dve, s_txt[b], 32 * (q + 1))
                    stats_of(beta, b, b, h, s_stat, s_mv, s_rstd_a, 1.0 + EPS, EPS * EPS)
                elif name == "norm":
                    normalise(beta, b, b, h, xn, s_rstd, s_norm, s_mv)
                elif name == "statsf":
                    wait(dve, s_hf, 2 * beta + 2)
                    stats_of(beta, b, 2 + b, hf, s_statf, s_mvf, s_rstdf_a, 1.0, EPS)
                elif name == "normf":
                    normalise(beta, b, 2 + b, hf, xnf, s_rstdf, s_normf, s_mvf)
                elif name == "mixA":
                    split_A(beta, bank(name, b), s_mixhi, mixA_hi[:, :], mixA_lo[:, :], s_mixlo)
                elif name == "mixC":
                    split_C(beta, bank(name, b), s_mixc0, mixC, s_mixc)
                elif name == "conv":
                    conv_taps(beta, k)
                elif name == "actlo":
                    act_lo_of(beta, k)
                elif name == "softplus":
                    scan_1(q, k)
                elif name == "scan":
                    scan_2(q, k)
                elif name == "stateslo":
                    us_lo(q)
                elif name == "us":
                    evac_us(beta, b, k)
                elif name == "mlpA":
                    split_A(beta, bank(name, b), s_mlphi, mlpA_hi[:, b, :], mlpA_lo[:, b, :], s_mlplo)
                elif name == "mlpC":
                    split_C(beta, bank(name, b), s_mlpc0, mlpC[:, b, :], s_mlpc)
                elif name == "route":
                    evac_route(beta, b)
                elif name == "pick":
                    gates_1(beta)
                elif name == "weigh":
                    gates_2(beta)
                else:
                    raise AssertionError(name)

            def iteration(i, mlp, carry, mix, pooling):
                for s in range(SLOTS):
                    for name, b, k in steps(DVE_STEPS, s):
                        if name in ("hidden", "lo"):
                            work = hidden if name == "hidden" else hidden_lo
                            if mlp and s > 0:
                                work(i, s - 1)
                            elif carry:
                                work(i - 1, SLOTS - 1)
                        elif name == "result":
                            if b == 1 and carry:
                                result(2 * i - 1, 1)
                            elif b == 0 and mlp:
                                result(2 * i, 0)
                        elif name == "pool":
                            if pooling:
                                pool_chunk(i + 2, k)
                        elif pair_of(i, name, b, mlp, mix) is not None:
                            step(name, b, k, pair_of(i, name, b, mlp, mix))

            iterations(dve, iteration, FULL)
            hidden(NP - 1, SLOTS - 1)
            hidden_lo(NP - 1, SLOTS - 1)
            result(2 * NP - 1, 1)

        @block.tensor
        def _(pe):
            def mm(dst, w, m, start, stop):
                return nc.tensor.matmul(dst, w, m, start=start, stop=stop)

            pe.wait_ge(s_small, 16 * SMALL_COUNT)
            pe.wait_ge(s_const, 1)
            for f in range(KE):
                nc.tensor.transpose(gu[:, f, 0:P], wxp_st[:, f, 0:P], ident[:, :])
                nc.tensor.transpose(gu[0:R, f, P:2 * P], wxp_st[:, f, P:D], ident[:, :]).then_inc(s_prep_pe, 1)
            for e in range(KE):
                mm(prep[:, e:e + 1], win_st[0][:, P * e:P * (e + 1)], lnb[:, 0:1], True, False)
                last = mm(prep[:, e:e + 1], win_st[1][0:R, P * e:P * (e + 1)], lnb[0:R, 1:2], False, True)
            last.then_inc(s_prep_pe, 1)
            pe.wait_ge(s_prep_act, KE)
            for f in range(KE):
                mm(gu[:, f, 0:D], wxpT[0][:, P * f:P * (f + 1)], wout_st[0], True, False)
                mm(gu[:, f, 0:D], wxpT[1][:, P * f:P * (f + 1)], wout_st[1], False, True).then_inc(s_prep_pe, 1)
            pe.wait_ge(s_prep_dve, 2)
            nc.tensor.transpose(prep[:, 0:NST], wus_st[:, 0:P], ident[0:NST, 0:NST])
            nc.tensor.transpose(prep[0:R, NST:2 * NST], wus_st[:, P:D], ident[0:NST, 0:NST]).then_inc(s_prep_pe, 1)
            pe.wait_ge(s_usl, 1)
            for b in range(2):
                mm(acc[:, b, 0:D], uslT[0][:, b, :], wout_st[0], True, False)
                mm(acc[:, b, 0:D], uslT[1][:, b, :], wout_st[1], False, True).then_inc(s_prep_pe, 1)
            pe.wait_ge(s_prep_w, 1)

            def up_step(i, s, k):
                n, b, t = SLOTS * i + s, s // T, s % T
                if k == 0:
                    if t == 0:
                        wait(pe, s_mlplo, 2 * i + b + 1)
                        wait(pe, s_mlpc, 2 * i + b + 1)
                    wait(pe, s_sil, n)
                else:
                    wait(pe, s_hid, n - 1)
                at, done = ((gate_col(t), s_g), (up_col(t), s_u))[k]
                dst = gu[:, 1 + s % 2 if k else 0, 0:L]
                c = slice(at, at + P)
                mm(dst, upA_hi[:, c], mlpA_hi[:, b, :], True, False)
                mm(dst, upA_lo[:, c], mlpA_hi[:, b, :], False, False)
                mm(dst, upA_hi[:, c], mlpA_lo[:, b, :], False, False)
                mm(dst, upC_hi[:, c], mlpC[:, b, :], False, False)
                mm(dst, upC_lo[:, c], mlpC[:, b, :], False, True).then_inc(done, 1)

            def down_step(i, s):
                n, t = SLOTS * i + s, s % T
                wait(pe, s_lo, n + 1)
                if t == 0:
                    wait(pe, s_res, 2 * i + s // T)
                for m in range(3):
                    tok = slice(TM * m, TM * (m + 1))
                    hi = (acc[0:TM, m, 0:2 * D], hid_hi[:, s % 3, tok], down[:, t, :])
                    lo = (acc[0:TM, m, 0:D], hid_lo[:, s % 3, tok], down[:, t, 0:D])
                    if t < T - 1:
                        mm(*hi, t == 0, False)
                        last = mm(*lo, False, False)
                    else:
                        mm(*lo, False, False)
                        last = mm(*hi, False, True)
                last.then_inc(s_down, 1)

            def transposes(dst, src, at):
                for m in range(3):
                    last = nc.tensor.transpose(dst[:, TM * m:TM * (m + 1)], src[0:TM, m, at:at + P], ident[0:TM, 0:TM])
                return last

            def job(name, b, k, q):
                beta = 2 * q + b
                to = bank(name, b, k)
                if name == "pool":
                    wait(pe, s_pooled, CHUNKS * (q + 1))
                    for m, (t0, t1) in enumerate(((0, TM), (TM, IMG))):
                        dst = to[0:t1 - t0, D * m:D * (m + 1)]
                        mm(dst, pooled[:, b, t0:t1], chan[:, 2 * b, :], True, False)
                        last = mm(dst, pooled[:, b + 1, t0:t1], chan[:, 2 * b + 1, :], False, True)
                    last.then_inc(s_job["pool"], 1)
                elif name in ("mixA", "mixC"):
                    wait(pe, s_dup, beta + 1)
                    transposes(to, xn, 0 if name == "mixA" else P).then_inc(s_job[name], 1)
                elif name in ("mlpA", "mlpC"):
                    wait(pe, s_dupf, beta + 1)
                    transposes(to, xnf, 0 if name == "mlpA" else P).then_inc(s_job[name], 1)
                elif name == "in":
                    if k == 0:
                        wait(pe, s_mixlo, beta + 1)
                        wait(pe, s_mixc, beta + 1)
                    c = slice(P * k, P * (k + 1))
                    dst = to[:, 0:L]
                    mm(dst, inA_hi[:, c], mixA_hi[:, :], True, False)
                    mm(dst, inA_lo[:, c], mixA_hi[:, :], False, False)
                    mm(dst, inA_hi[:, c], mixA_lo[:, :], False, False)
                    mm(dst, inC_hi[:, c], mixC[:, :], False, False)
                    mm(dst, inC_lo[:, c], mixC[:, :], False, True).then_inc(s_job["in"], 1)
                elif name == "act":
                    wait(pe, s_actlo, 3 * beta + 3)
                    for at, m in enumerate((2,) if k else (0, 1)):
                        tok = slice(TM * m, TM * (m + 1))
                        dst = to[0:TM, NX * at:NX * (at + 1)]
                        for f in range(KE):
                            mm(dst, act_hi[:, f, tok], actw_hi[:, f, :], f == 0, False)
                            mm(dst, act_hi[:, f, tok], actw_lo[:, f, :], False, False)
                            last = mm(dst, act_lo[:, f, tok], actw_hi[:, f, :], False, f == KE - 1)
                    last.then_inc(s_job["act"], 1)
                elif name in ("dt", "ds"):
                    wait(pe, s_zs, 4 * (q + 1))
                    at = 0 if name == "dt" else 2 * NST
                    for m in range(3):
                        last = nc.tensor.transpose(to[0:2 * NST, TM * m:TM * (m + 1)], zs[0:TM, m, at:at + 2 * NST],
                                                   ident[0:TM, 0:TM])
                    last.then_inc(s_job[name], 1)
                elif name == "us":
                    wait(pe, s_uslo, q + 1)
                    wait(pe, s_ushi, 2 * q + 2)
                    for at, m in enumerate((2,) if k else (0, 1)):
                        last = mm(to[0:TM, D * at:D * (at + 1)], us[:, TM * m:TM * (m + 1)], usw[:, b, :], True, True)
                    last.then_inc(s_job["us"], 1)
                elif name == "route":
                    wait(pe, s_mlplo, beta + 1)
                    wait(pe, s_mlpc, beta + 1)
                    for m in range(3):
                        tok = slice(TM * m, TM * (m + 1))
                        dst = to[0:TM, 32 * m:32 * (m + 1)]
                        mm(dst, mlpA_hi[:, b, tok], routeA[:, :], True, False)
                        mm(dst[:, 0:16], mlpA_lo[:, b, tok], routeA[:, 0:16], False, False)
                        last = mm(dst, mlpC[:, b, tok], routeC[:, :], False, True)
                    last.then_inc(s_job["route"], 1)
                elif name == "gates":
                    wait(pe, s_gt, beta + 1)
                    for m in range(3):
                        last = nc.tensor.transpose(to[0:NE + 1, TM * m:TM * (m + 1)], gt[0:TM, m, :], ident[0:TM, 0:TM])
                    last.then_inc(s_job["gates"], 1)

                else:
                    raise AssertionError(name)

            def wait_for_bank(i, now, mlp, mix):
                at = JOBS.index(now)
                earlier = [(j, i, mlp, mix) for j in reversed(JOBS[at % 2:at:2])]
                if not (isinstance(i, int) and i < 0):
                    earlier += [(j, i - 1, True, True) for j in reversed(JOBS[at % 2::2])]
                for (name, b, k), of, has_mlp, has_mix in earlier:
                    q = pair_of(of, name, b, has_mlp, has_mix)
                    if q is not None:
                        wait(pe, *evacuated(name, b, k, q))
                        return

            def iteration(i, mlp, carry, mix, pooling):
                for s in range(SLOTS):
                    for name, b, k in steps(PE_STEPS, s):
                        if name in ("gate", "up"):
                            if mlp:
                                up_step(i, s, int(name == "up"))
                        elif name == "down":
                            if mlp and s >= 2:
                                down_step(i, s - 2)
                            elif carry:
                                down_step(i - 1, SLOTS - 2 + s)
                        elif pair_of(i, name, b, mlp, mix) is not None:
                            wait_for_bank(i, (name, b, k), mlp, mix)
                            job(name, b, k, pair_of(i, name, b, mlp, mix))
                if isinstance(i, int) and i == -1:
                    pe.wait_ge(s_stage_lo, PIECES)

            iterations(pe, iteration, FULL)
            down_step(NP - 1, SLOTS - 2)
            down_step(NP - 1, SLOTS - 1)


_OUT = ((64, 324, 192), "float32")
_INS = ["x", "txt", "L0_tok_channel_weights"] + ["L0_attn_" + n for n in (
    "ln_g", "ln_b", "W_in", "b_in", "W_conv", "b_conv", "W_xp", "b_xp", "W_dt", "b_dt", "W_us", "b_us", "W_out", "b_out")] + [
    "L0_ffn_" + n for n in ("router_w", "w_gate", "w_up", "w_down", "ws_gate", "ws_up", "ws_down", "sg_w", "sg_b")]


def kernel(**inputs):
    import numpy as _np
    import concourse.bacc as _bacc
    from concourse import mybir as _mybir
    from concourse.bass_utils import run_bass_kernel_spmd as _run

    nc = _bacc.Bacc("TRN2", target_bir_lowering=False, num_devices=1)
    arrays, args = {}, []
    for name in _INS:
        a = _np.ascontiguousarray(inputs[name])
        arrays[f"in_{name}_dram"] = a
        args.append(nc.dram_tensor(f"in_{name}_dram", a.shape, _mybir.dt.from_np(a.dtype), kind="ExternalInput").ap())
    shape = (inputs["x"].shape[0],) + _OUT[0][1:]
    result = nc.dram_tensor("out_0_dram", shape, _mybir.dt.from_np(_np.dtype(_OUT[1])), kind="ExternalOutput").ap()
    build(nc, *args, result)
    r = _run(nc, [arrays], core_ids=[0])
    return r.results[0]["out_0_dram"]
```

```python
from contextlib import ExitStack

import concourse.bass as bass
from concourse import mybir

F32 = mybir.dt.float32
F32R = mybir.dt.float32r
U32 = mybir.dt.uint32
ALU = mybir.AluOpType
ACT = mybir.ActivationFunctionType
AX_X = mybir.AxisListType.X

P = 128
SLOTS = 36
RING = 7
POOL_BEFORE = 12
CHUNKS = 21


PE_STEPS = (
    "pool:0 gate up down",
    "gate up down",
    "gate up out:1:0 out:1:1 down",
    "gate up us:1:0 us:1:1 down",
    "gate mixA:0 mixC:0 up down",
    "gate up pool:1 down",
    "gate up down",
    "gate in:0:0 up in:0:1 down",
    "gate in:0:2 up down",
    "gate up down mlpA:1 mlpC:1",
    "gate up down",
    "gate mixA:1 mixC:1 up down",
    "gate up in:1:0 route:1 down",
    "gate act:0:0 up down",
    "gate act:0:1 in:1:1 in:1:2 up down gates:1",
    "gate up down",
    "gate up down",
    "gate act:1:0 act:1:1 up down",
    "gate up dt down",
    "gate ds up down",
    "gate out:0:0 up down",
    "gate up down",
    "gate up down",
    "gate up down",
    "gate up out:0:1 down",
    "gate up down",
    "gate us:0:0 us:0:1 up down",
    "gate up down",
    "gate up down",
    "gate mlpA:0 mlpC:0 up down",
    "gate up down",
    "gate route:0 up down",
    "gate up down",
    "gate gates:0 up down",
    "gate up down",
    "gate up down",
)
ACT_STEPS = (
    "pool:0 silu hi",
    "silu out:1 hi",
    "silu double:0 hi",
    "silu hi",
    "silu hi mixA:0",
    "silu mixC:0 hi",
    "silu hi pool:1 doublef:1",
    "silu hi in:0:0",
    "silu in:0:1 convsilu:0:0 hi in:0:2",
    "silu double:1 mlpA:1 hi mlpC:1",
    "silu hi mixA:1 mixC:1",
    "silu convsilu:0:1 hi",
    "silu convsilu:0:2 hi in:1:0 act:0:0",
    "silu hi",
    "silu gtanh:1 act:0:1 in:1:1 in:1:2 hi convsilu:1:0",
    "silu gates:1 hi convsilu:1:1 convsilu:1:2",
    "silu hi",
    "silu act:1:0 act:1:1 hi",
    "silu hi dt",
    "silu exp ln out:0 ds exp2 hi",
    "silu tanh hi",
    "silu hi",
    "silu hi",
    "silu hi",
    "silu hi",
    "silu states hi",
    "silu hi",
    "silu hi",
    "silu doublef:0 hi",
    "silu mlpA:0 mlpC:0 hi",
    "silu hi",
    "silu hi gtanh:0",
    "silu hi",
    "silu gates:0 hi",
    "silu hi",
    "silu hi",
)
DVE_STEPS = (
    "hidden stats:0 lo",
    "hidden norm:0 lo",
    "hidden result:1:0 result:1:1 lo",
    "hidden us:1:0 us:1:1 lo",
    "hidden statsf:1 mixA:0 lo",
    "hidden mixC:0 lo",
    "hidden pool:0 normf:1 lo",
    "hidden pool:1 pool:2 stats:1 lo conv:0:0",
    "hidden norm:1 lo",
    "hidden conv:0:1 mlpA:1 lo",
    "hidden mlpC:1 conv:0:2 lo mixC:1",
    "hidden mixA:1 lo",
    "hidden actlo:0:0 actlo:0:1 actlo:0:2 route:1 lo pool:3",
    "hidden pick:1 conv:1:0 pool:4 pool:5 lo",
    "hidden weigh:1 conv:1:1 lo",
    "hidden conv:1:2 lo actlo:1:0 actlo:1:1 actlo:1:2",
    "hidden lo",
    "hidden pool:6 pool:7 lo pool:8 pool:9",
    "hidden pool:10 pool:11 lo",
    "hidden softplus:0 pool:12 softplus:1 lo",
    "hidden result:0:0 lo",
    "hidden scan:0 lo",
    "hidden scan:1 lo",
    "hidden scan:2 lo",
    "hidden scan:3 lo",
    "hidden stateslo result:0:1 lo",
    "hidden us:0:0 us:0:1 lo",
    "hidden statsf:0 lo pool:13 normf:0",
    "hidden lo",
    "hidden pool:14 mlpC:0 lo",
    "hidden pool:15 mlpA:0 lo pool:16 route:0",
    "hidden pick:0 lo",
    "hidden weigh:0 pool:17 lo",
    "hidden pool:18 lo",
    "hidden pool:19 lo pool:20",
    "hidden lo",
)
POOL_STEPS = (
    "rstd:0 gated",
    "gated",
    "gated",
    "gated",
    "gated",
    "gated rstdf:1",
    "gated",
    "gated rstd:1",
    "gated",
    "gated",
    "gated",
    "gated",
    "gated",
    "gated addy:0:0 addy:0:1",
    "gated",
    "gated",
    "gated",
    "gated addy:1:0 addy:1:1",
    "gated",
    "gated scanin",
    "gated",
    "gated",
    "gated",
    "gated",
    "gated",
    "gated",
    "gated rstdf:0",
    "gated",
    "gated",
    "gated",
    "gated",
    "gated",
    "gated",
    "gated",
    "gated",
    "gated",
)
SP_STEPS = (
    "text:1 load:0 load:1 load:2 store:1 load:3 gates:1 load:4 load:5 "
    "load:6 load:7 load:8 load:9 load:10 text:0 store:0 load:11 load:12 "
    "load:13 load:14 load:15 gates:0 load:16 load:17 load:18 load:19 load:20",
)

TAIL = ("us", "statsf", "rstdf", "normf", "doublef", "mlpA", "mlpC", "route", "pick", "gtanh", "weigh", "gates")

def build(nc, x, txt, cw, ln_g, ln_b, W_in, b_in, W_conv, b_conv, W_xp, b_xp, W_dt, b_dt, W_us, b_us,
          W_out, b_out, router_w, w_gate, w_up, w_down, ws_gate, ws_up, ws_down, sg_w, sg_b, out):
    B, C, HW, _ = x.shape
    D = cw.shape[1]
    PATCH = 16
    G = HW // PATCH
    IMG = G * G
    L = out.shape[1]
    TM = L // 3
    E1 = W_in.shape[1]
    KE = E1 // P
    NST = W_dt.shape[1]
    NX = D + 2 * NST
    R = D - P
    NE = router_w.shape[1]
    RT = NE * w_gate.shape[2] // P
    ST = ws_gate.shape[1] // P
    T = RT + ST
    NP = B // 2
    CH = 2 * G * PATCH
    EPS = 1e-5
    assert 3 * TM == L and L - IMG == txt.shape[1] and 2 * T == SLOTS and NP >= 5 and C == 12

    x_rows = x.rearrange("b c h w -> (b c) h w")
    routed_gates_dram = nc.dram_tensor("routed_gates", [16, L], F32).ap()

    ctx = ExitStack()
    with ctx:
        def sb(name, shape, dt=F32):
            return ctx.enter_context(nc.sbuf_tensor(name, shape, dt))

        def sem(name):
            return ctx.enter_context(nc.semaphore(name))

        upA_hi = sb("upA_hi", [P, 2 * T * P], F32R)
        upA_lo = sb("upA_lo", [P, 2 * T * P], F32R)
        upC_hi = sb("upC_hi", [P, 2 * T * P], F32R)
        upC_lo = sb("upC_lo", [P, 2 * T * P], F32R)
        down = sb("down", [P, T, 2 * D], F32R)
        inA_hi = sb("inA_hi", [P, E1], F32R)
        inA_lo = sb("inA_lo", [P, E1], F32R)
        inC_hi = sb("inC_hi", [P, E1], F32R)
        inC_lo = sb("inC_lo", [P, E1], F32R)
        actw_hi = sb("actw_hi", [P, KE, NX], F32R)
        actw_lo = sb("actw_lo", [P, KE, NX], F32R)
        usw = sb("usw", [P, 2, D], F32R)
        routeA = sb("routeA", [P, 32], F32R)
        routeC = sb("routeC", [P, 32], F32R)
        chan = sb("chan", [P, 4, D])
        ident = sb("ident", [P, P])
        taps = sb("taps", [P, KE, 4])
        col = sb("col", [P, 24])
        lnb = sb("lnb", [P, 4])
        biota = sb("biota", [P, NE])
        khalf = sb("khalf", [32, L])
        power = sb("power", [P, 3])
        ring = sb("ring", [P, RING, CH])
        pooled = sb("pooled", [P, 3, IMG])
        h = sb("h", [P, 2, 3, D])
        hf = sb("hf", [P, 2, 3, D])
        res = sb("res", [P, 3, D])
        stats = sb("stats", [P, 4, 3, 6])
        mv = sb("mv", [P, 4, 3, 2])
        rstd = sb("rstd", [P, 4, 3])
        xn = sb("xn", [P, 3, 2 * P])
        xnf = sb("xnf", [P, 3, 2 * P])
        mlp_out = xnf[:, :, :].rearrange("p m d -> p (m d)")[:, 0:2 * L].rearrange("p (c l) -> p c l", c=2)
        mixA_hi = sb("mixA_hi", [P, L], F32R)
        mixA_lo = sb("mixA_lo", [P, L], F32R)
        mixC = sb("mixC", [P, L], F32R)
        mlpA_hi = sb("mlpA_hi", [P, 2, L], F32R)
        mlpA_lo = sb("mlpA_lo", [P, 2, L], F32R)
        mlpC = sb("mlpC", [P, 2, L], F32R)
        xin = sb("xin", [P, KE, 3 + L])
        conv = sb("conv", [P, KE, L])
        act_hi = sb("act_hi", [P, KE, L], F32R)
        act_lo = sb("act_lo", [P, KE, L], F32R)
        yz = sb("yz", [P, 3, NX])
        zs = sb("zs", [P, 3, 4 * NST])
        xn_st, yz_st = (a[0:32, :, :].rearrange("p m d -> p (m d)") for a in (xn, yz))
        sc = [conv[0:32, 0, :], conv[0:32, 1, :], conv[0:32, 2, :], xn_st[:, 0:L], xn_st[:, L:2 * L], yz_st[:, 0:L],
              yz_st[:, L:2 * L]]
        us = sb("us", [P, L], F32R)
        lg = sb("lg", [P, 3, 32])
        logit = sb("logit", [P, 3, 16])
        top = sb("top", [P, 3, 8])
        topi = sb("topi", [P, 3, 8], U32)
        topf = sb("topf", [P, 3, 8])
        gsc = sb("gsc", [P, 8, 3])
        pick = sb("pick", [P, 2, 3, 8])
        gt = sb("gt", [P, 3, 9])
        gs = sb("gs", [9, L])
        gate_bc = sb("gate_bc", [P, NE, L])
        alpha_bc = sb("alpha_bc", [P, 2, L])
        hid = sb("hid", [P, 3, L])
        hid_hi = sb("hid_hi", [P, 3, L], F32R)
        hid_lo = sb("hid_lo", [P, 3, L], F32R)
        gb_flat = gate_bc[:, :, :].rearrange("p e l -> p (e l)")
        PIECE = 4 * D
        stage = [gb_flat[:, PIECE * k:PIECE * (k + 1)] for k in range(3)]
        hf_flat = hf[:, :, :, :].rearrange("p b m d -> p (b m d)")
        win_st = [hf_flat[:, 0:E1], hf_flat[:, E1:2 * E1]]
        wout_st = [hf_flat[:, 2 * E1:2 * E1 + D], hf_flat[0:R, 2 * E1 + D:2 * E1 + 2 * D]]
        hid_flat = hid[:, :, :].rearrange("p s l -> p (s l)")
        wxp_st = hid_flat[:, 0:KE * (D + NST)].rearrange("p (k n) -> p k n", k=KE)
        wdt_st = hid_flat[:, KE * (D + NST):KE * NX].rearrange("p (k n) -> p k n", k=KE)
        wus_st = hid_flat[0:NST, KE * NX:KE * NX + D]
        woutf_st = res
        xnf_flat = xnf[:, :, :].rearrange("p m d -> p (m d)")
        wxpT = [xnf_flat[:, 0:E1], xnf_flat[0:R, E1:2 * E1]]
        al_flat = alpha_bc[:, :, :].rearrange("p b l -> p (b l)")
        uslT = [al_flat[:, 0:2 * P].rearrange("p (b c) -> p b c", b=2),
                al_flat[0:R, 2 * P:4 * P].rearrange("p (b c) -> p b c", b=2)]
        xn_flat = xn[:, :, :].rearrange("p m d -> p (m d)")
        bout_st = xn_flat[:, 0:D]
        uw = xn_flat[:, D:2 * D]
        rt_st = sb("rt_st", [P, 2, 16])
        wx_full = yz
        iota_i = conv[:, 0, :].bitcast(mybir.dt.int32)
        settled = sb("settled", [1, 1])
        binf = sb("binf", [P, KE])
        bconv = sb("bconv", [P, KE])
        sgbh = sb("sgbh", [P, 1])

        GA, GC, BIN, BCV, BDT, BDS, SGB, MHI, MLO = 0, 1, 4, 7, 13, 14, 15, 16, 17
        USC, XPC = 18, 20

        gu = ctx.enter_context(nc.psum_tensor("gu", [P, 4, 512], F32))
        acc = ctx.enter_context(nc.psum_tensor("acc", [P, 2, 512], F32))
        misc = ctx.enter_context(nc.psum_tensor("misc", [P, 2, 512], F32))
        prep = misc[:, 0, :]

        s_fold = sem("weights_to_fold_loaded")
        s_small = sem("small_weights_loaded")
        s_zeroed = sem("zeroed_for_loads")
        s_const = sem("constants_made")
        s_const_chain = sem("constants_chain")
        s_stage = [sem(f"stage_loaded{k}") for k in range(3)]
        s_stage_hi = sem("stage_hi_split")
        s_stage_lo = sem("stage_lo_split")
        s_prep_pe = sem("prep_products")
        s_prep_act = sem("prep_evacuated")
        s_prep_dve = sem("prep_vector_chain")
        s_usl = sem("state_weights_stacked")
        s_prep_w = sem("mixer_weights_ready")
        s_chunk = [sem(f"chunk_loaded{k}") for k in range(RING)]
        s_pooled = sem("chunk_pooled")
        s_txt = [sem(f"text_loaded{b}") for b in range(2)]
        s_job = {k: sem(f"{k}_product") for k in ("pool", "mixA", "mixC", "in", "act", "dt", "ds", "us", "mlpA", "mlpC",
                                                  "route", "gates", "out")}
        s_mlpout = sem("mlp_output_evacuated")
        s_tokens = sem("tokens_in_h")
        s_stat = sem("stats_chain")
        s_mv = sem("mean_var")
        s_rstd_a = sem("variance_scaled")
        s_rstd = sem("rstd")
        s_norm = sem("normalised")
        s_dup = sem("normalised_tail_doubled")
        s_mixhi, s_mixlo, s_mixc0, s_mixc = sem("mixA_hi_ready"), sem("mixA_lo_ready"), sem("mixC_hi_ready"), sem("mixC_ready")
        s_xin = sem("conv_input_ready")
        s_tap = sem("conv_taps")
        s_acthi = sem("act_hi_ready")
        s_actlo = sem("act_lo_ready")
        s_yz = sem("yz_evacuated")
        s_hy = sem("h_plus_y")
        s_zs = sem("zs_ready")
        s_dtev = sem("dt_evacuated")
        s_dsev = sem("ds_evacuated")
        s_exp1, s_ln, s_exp2, s_tanh1, s_tanhk = (sem(n) for n in ("exp_az", "ln_w", "exp_half_dt", "tanh_half_dt", "tanh_half_kdt"))
        s_scan = sem("scan_chain")
        s_scan_w = sem("scan_w")
        s_dtdone = sem("dt_ready")
        s_kd = sem("kdt_ready")
        s_ab = sem("scan_inputs")
        s_usf = sem("us_float")
        s_ushi = sem("us_hi")
        s_uslo = sem("us_lo")
        s_hf = sem("hf_ready")
        s_statf = sem("mlp_stats_chain")
        s_mvf, s_rstdf_a, s_rstdf, s_normf, s_dupf = (sem(n) for n in ("mlp_mean_var", "mlp_variance_scaled", "mlp_rstd", "mlp_normalised",
                                                                  "mlp_normalised_doubled"))
        s_mlphi, s_mlplo, s_mlpc0, s_mlpc = sem("mlpA_hi_ready"), sem("mlpA_lo_ready"), sem("mlpC_hi_ready"), sem("mlpC_ready")
        s_lg = sem("logits_evacuated")
        s_gate = sem("gates_chain")
        s_diff = sem("logit_difference")
        s_gtanh = sem("gate_tanh")
        s_gt = sem("gates_token_major")
        s_gs = sem("gates_feature_major")
        s_gdram = sem("gates_in_dram")
        s_gbc = sem("gates_loaded")
        s_g, s_u, s_sil, s_gated, s_hid, s_hi, s_lo, s_down = (sem(n) for n in (
            "gate_projected", "up_projected", "silu_done", "gated", "hidden_ready", "hidden_hi", "hidden_lo", "down_projected"))
        s_res1 = sem("result_half")
        s_res = sem("result_ready")
        s_out = sem("result_stored")

        FOLD_COUNT, SMALL_COUNT = 25, 14

        SCAN_STEPS = 14

        block = ctx.enter_context(nc.Block())

        def wait(eng, s, value):
            if isinstance(value, int) and value <= 0:
                return
            eng.wait_ge(s, value)

        def parts(i):
            return dict(mlp=i >= 0, carry=i >= 1, mix=-1 <= i <= NP - 2, pooling=i <= NP - 3)

        def iterations(eng, body, loop_to):
            for i in (-1, 0):
                body(i, **parts(i))
            with eng.Fori(1, loop_to + 1) as i:
                body(i, **parts(1))
            for i in range(loop_to + 1, NP):
                body(i, **parts(i))

        FULL = NP - 3

        def steps(table, slot):
            for word in table[slot].split():
                name, *numbers = word.split(":")
                if name == "pool" and table is DVE_STEPS or name in ("scan", "softplus", "load"):
                    numbers = [0, *numbers]
                yield (name, *(int(n) for n in numbers), *[0] * (2 - len(numbers)))

        def pair_of(i, name, b, carry, mlp, mix):
            if name in ("out", "result"):
                return (i - 1 if carry else None) if b == 1 else (i if mlp else None)
            if name in TAIL and b == 1:
                return i if mlp else None
            return i + 1 if mix else None

        def evacuated(name, b, k, q):
            beta = 2 * q + b
            return {
                "pool": (s_tokens, beta + 1), "mixA": (s_mixlo, beta + 1), "mixC": (s_mixc, beta + 1),
                "in": (s_xin, 3 * beta + k + 1), "act": (s_yz, 2 * beta + k + 1), "dt": (s_dtev, q + 1), "ds": (s_dsev, q + 1),
                "us": (s_hf, 2 * beta + k + 1), "mlpA": (s_mlplo, beta + 1), "mlpC": (s_mlpc, beta + 1),
                "route": (s_lg, beta + 1), "gates": (s_gs, beta + 1), "out": (s_res, 2 * beta + k + 1),
            }[name]

        JOBS = [step for slot in range(SLOTS) for step in steps(PE_STEPS, slot) if step[0] not in ("gate", "up", "down")]

        def bank(name, b=0, k=0):
            return misc[:, JOBS.index((name, b, k)) % 2, :]

        PIECES = 17
        PIECE_LOADS = [16] * 6 + [32] * 6 + [16] * 5

        def piece_loaded(n):
            return sum(PIECE_LOADS[m] for m in range(n % 3, n + 1, 3))

        def piece_at(n):
            if n < 12:
                hi, lo = ((upA_hi, upA_lo), (upC_hi, upC_lo))[n // 6]
                k = n % 6
                at = {0: 0, 1: PIECE, 2: 4 * PIECE, 3: 2 * PIECE, 4: 3 * PIECE, 5: 5 * PIECE}[k]
                return hi[:, at:at + PIECE], lo[:, at:at + PIECE], PIECE
            tiles = 4 if n < 16 else 2
            t = 4 * (n - 12)
            return down[:, t:t + tiles, 0:D], down[:, t:t + tiles, D:2 * D], tiles * D

        def pieces_of_lo(n):
            hi, lo, w = piece_at(n)
            if n < 12:
                return [(hi, lo, slice(0, w))]
            return [(hi[:, :, P:D], lo[:, :, 0:R], slice(P, D)), (hi[:, :, 0:P], lo[:, :, R:D], slice(0, P))]

        def gate_col(t):
            return P * t if t < RT else 4 * PIECE + P * (t - RT)

        def up_col(t):
            return 2 * PIECE + P * t if t < RT else 5 * PIECE + P * (t - RT)

        @block.sync
        def _(sp):
            def load_chunk(q, c):
                tile, j = divmod(c, G // 2)
                for k in range(2):
                    row = PATCH * (2 * j + k)
                    sp.dma_start(ring[:, c % RING, HW * k:HW * (k + 1)],
                                 x_rows[bass.ds(2 * C * q + 8 * tile, 8), row:row + PATCH, :]).then_inc(s_chunk[c % RING], 16)

            def load_text(q, b):
                src = txt[bass.ds(2 * q + b, 1), :, :].rearrange("b t d -> (b t) d")
                cut = 2 * TM - IMG
                sp.dma_start(h[IMG - TM:TM, b, 1, :], src[0:cut, :]).then_inc(s_txt[b], 16)
                sp.dma_start(h[0:TM, b, 2, :], src[cut:cut + TM, :]).then_inc(s_txt[b], 16)

            def store(beta):
                wait(sp, s_res, 2 * beta + 2)
                dst = out[bass.ds(beta, 1), :, :].rearrange("b (m p) d -> p (b m) d", p=TM)
                sp.dma_start(dst, res[0:TM, :, :]).then_inc(s_out, 16)

            def spread_gates(beta, b):
                if isinstance(beta, int) and beta == 0:
                    sp.wait_ge(s_stage_lo, PIECES)
                    sp.wait_ge(s_prep_w, 1)
                wait(sp, s_gs, beta + 1)
                wait(sp, s_gated, T * (beta - 1) + RT)
                sp.dma_start(routed_gates_dram[0:NE + 1, :], gs[:, :]).then_inc(s_gdram, 16)
                wait(sp, s_gdram, 16 * (beta + 1))
                sp.dma_start(gate_bc[:, :, :].rearrange("p e l -> p (e l)"),
                             routed_gates_dram[0:NE, :].rearrange("(o e) l -> o (e l)", o=1).broadcast_to([P, NE * L])
                             ).then_inc(s_gbc, 16)
                sp.dma_start(alpha_bc[:, b, :], routed_gates_dram[NE:NE + 1, :].broadcast_to([P, L])).then_inc(s_gbc, 16)

            def iteration(i, mlp, carry, mix, pooling):
                more = pooling and (not isinstance(i, int) or i <= NP - 4)
                for name, b, c in steps(SP_STEPS, 0):
                    if name == "store" and b == 1 and carry:
                        store(2 * i - 1)
                    elif name == "store" and b == 0 and mlp:
                        store(2 * i)
                    elif name == "gates" and b == 1 and mlp:
                        spread_gates(2 * i + 1, 1)
                    elif name == "gates" and b == 0 and mix:
                        spread_gates(2 * i + 2, 0)
                    elif name == "text" and b == 1 and mlp and mix:
                        wait(sp, s_hf, 2 * (2 * i + 1) + 2)
                        load_text(i + 1, 1)
                    elif name == "text" and b == 0 and pooling:
                        if mix:
                            wait(sp, s_hf, 2 * (2 * i + 2) + 2)
                        load_text(i + 2, 0)
                    elif name == "load" and (pooling if c + RING < CHUNKS else more):
                        wait(sp, s_pooled, CHUNKS * (i + 2) + c + 1)
                        load_chunk(*((i + 2, c + RING) if c + RING < CHUNKS else (i + 3, c + RING - CHUNKS)))

            for c in range(RING):
                load_chunk(0, c)
            pieces = []
            for part in range(2):
                for w, ws in ((w_gate, ws_gate), (w_up, ws_up)):
                    rows = slice(0, P) if part == 0 else slice(P, D)
                    pieces += [(part, w[0:4, rows, :].rearrange("e d n -> d e n")), (part, w[4:8, rows, :].rearrange("e d n -> d e n")),
                               (part, ws[rows, :])]
            wd = w_down.rearrange("e n d -> (e n) d")
            pieces += [(2, wd[4 * P * k:4 * P * (k + 1), :].rearrange("(t p) d -> p t d", p=P)) for k in range(3)]
            pieces += [(2, ws_down[0:4 * P, :].rearrange("(t p) d -> p t d", p=P)),
                       (2, ws_down[4 * P:6 * P, :].rearrange("(t p) d -> p t d", p=P))]

            def load_piece(n):
                part, src = pieces[n]
                wait(sp, s_stage_lo, n - 2)
                dst = stage[n % 3]
                if len(src.shape) == 3:
                    dst = dst[:, 0:src.shape[1] * D].rearrange("p (e n) -> p e n", n=D)
                if part == 1:
                    sp.dma_start(dst[0:R], src).then_inc(s_stage[n % 3], 16)
                    sp.dma_start(dst[R:P], src).then_inc(s_stage[n % 3], 16)
                else:
                    sp.dma_start(dst, src).then_inc(s_stage[n % 3], 16)

            for n in range(3):
                load_piece(n)
            iteration(-2, **parts(-2))
            load_text(0, 1)
            for n in range(3, PIECES):
                load_piece(n)
            iterations(sp, iteration, NP - 4)
            store(2 * NP - 1)
            wait(sp, s_out, 16 * 2 * NP)

        @block.gpsimd
        def _(pool):
            pool.memset(chan[:, :, :], 0.0).then_inc(s_zeroed, 1)
            pool.memset(woutf_st[:, :, :], 0.0).then_inc(s_zeroed, 1)
            pool.memset(bout_st, 0.0).then_inc(s_zeroed, 1)
            pool.memset(rt_st[:, :, :], 0.0).then_inc(s_zeroed, 1)
            pool.memset(ident[:, :], 0.0).then_inc(s_const_chain, 1)
            pool.wait_ge(s_const_chain, 1)
            pool.affine_select(out=ident[:, :], in_=ident[:, :], compare_op=ALU.not_equal, fill=1.0, base=0,
                               pattern=[[-1, P]], channel_multiplier=1).then_inc(s_const, 1)
            pool.memset(col[:, MHI:MHI + 1], 1.0).then_inc(s_const_chain, 1)
            pool.memset(col[:, MLO:MLO + 1], 1.0).then_inc(s_const_chain, 1)
            pool.wait_ge(s_const_chain, 3)
            pool.affine_select(out=col[:, MHI:MHI + 1], in_=col[:, MHI:MHI + 1], compare_op=ALU.is_ge, fill=0.0,
                               base=63, pattern=[[0, 1]], channel_multiplier=-1).then_inc(s_const_chain, 1)
            pool.affine_select(out=col[:, MLO:MLO + 1], in_=col[:, MLO:MLO + 1], compare_op=ALU.is_ge, fill=0.0,
                               base=-64, pattern=[[0, 1]], channel_multiplier=1).then_inc(s_const_chain, 1)
            pool.wait_ge(s_const_chain, 5)
            pool.affine_select(out=col[:, MHI:MHI + 1], in_=col[:, MHI:MHI + 1], compare_op=ALU.not_equal, fill=1.0,
                               base=-96, pattern=[[0, 1]], channel_multiplier=1).then_inc(s_const, 1)
            pool.affine_select(out=col[:, MLO:MLO + 1], in_=col[:, MLO:MLO + 1], compare_op=ALU.not_equal, fill=0.0,
                               base=-96, pattern=[[0, 1]], channel_multiplier=1).then_inc(s_const, 1)
            pool.iota(iota_i[:, :], pattern=[[-1, L]], base=L - 1, channel_multiplier=0).then_inc(s_const_chain, 1)
            pool.wait_ge(s_const_chain, 6)
            pool.tensor_copy(khalf[:, :], iota_i[0:32, :]).then_inc(s_const_chain, 1)
            pool.tensor_copy(biota[:, :], iota_i[:, L - NE:L]).then_inc(s_const_chain, 1)
            pool.wait_ge(s_const_chain, 8)
            pool.tensor_scalar(khalf[:, :], khalf[:, :], 0.5, None, ALU.mult).then_inc(s_const, 1)
            pool.tensor_scalar(biota[:, :], biota[:, :], -1.0, float(NE - 1), ALU.mult, ALU.add).then_inc(s_const, 1)
            pool.memset(power[:, :], -0.5).then_inc(s_const, 1)
            pool.memset(xin[:, :, 0:3], 0.0).then_inc(s_const, 1)

            def gate_step(i, s):
                n, b, t = SLOTS * i + s, s // T, s % T
                wait(pool, s_sil, n + 1)
                buf = hid[:, s % 3, :]
                if t == 0:
                    wait(pool, s_gbc, 32 * (2 * i + b + 1))
                if t < RT:
                    lo_e, hi_e = (P * t) // D, (P * t + P - 1) // D
                    if lo_e == hi_e:
                        pool.tensor_tensor(buf, buf, gate_bc[:, lo_e, :], ALU.mult).then_inc(s_gated, 1)
                    else:
                        pool.tensor_tensor(hid[0:64, s % 3, :], hid[0:64, s % 3, :], gate_bc[0:64, lo_e, :], ALU.mult)
                        wait(pool, s_gated, n)
                        pool.tensor_tensor(hid[64:P, s % 3, :], hid[64:P, s % 3, :], gate_bc[64:P, hi_e, :],
                                           ALU.mult).then_inc(s_gated, 1)
                        wait(pool, s_gated, n + 1)
                else:
                    pool.tensor_tensor(buf, buf, alpha_bc[:, b, :], ALU.mult).then_inc(s_gated, 1)

            def rstd_of(beta, k, ready, done):
                wait(pool, ready, beta + 1)
                pool.tensor_tensor(rstd[0:TM, k, :], rstd[0:TM, k, :], power[0:TM, :], ALU.pow).then_inc(done, 1)

            def add_y(beta, b, k):
                wait(pool, s_yz, 2 * beta + k + 1)
                m = slice(0, 2) if k == 0 else slice(2, 3)
                pool.tensor_tensor(h[0:TM, b, m, :], h[0:TM, b, m, :], yz[0:TM, m, 0:D], ALU.add).then_inc(s_hy, 1)
                pool.tensor_copy(
                    zs[0:TM, m, :].rearrange("p m (k b n) -> p m k b n", k=2, b=2)[:, :, :, b, :],
                    yz[0:TM, m, D:NX].rearrange("p m (k n) -> p m k n", k=2)).then_inc(s_zs, 1)

            def iteration(i, mlp, carry, mix, pooling):
                for s in range(SLOTS):
                    for name, b, k in steps(POOL_STEPS, s):
                        if name == "gated":
                            if mlp:
                                gate_step(i, s)
                            continue
                        q = pair_of(i, name, b, carry, mlp, mix)
                        if q is None:
                            continue
                        beta = 2 * q + b
                        if name == "rstd":
                            rstd_of(beta, b, s_rstd_a, s_rstd)
                        elif name == "rstdf":
                            rstd_of(beta, 2 + b, s_rstdf_a, s_rstdf)
                        elif name == "addy":
                            add_y(beta, b, k)
                        elif name == "scanin":
                            wait(pool, s_exp2, q + 1)
                            wait(pool, s_scan, SCAN_STEPS * q + 3)
                            pool.tensor_tensor(sc[5], sc[6], sc[6], ALU.mult).then_inc(s_ab, 1)
                            wait(pool, s_dsev, q + 1)
                            pool.tensor_tensor(sc[2], sc[2], sc[6], ALU.mult).then_inc(s_ab, 1)
                        else:
                            raise AssertionError(name)

            iterations(pool, iteration, FULL)

        @block.scalar
        def _(act):
            loads = []

            def load(dst, src, loaded=s_fold):
                act.dma_start(dst, src, allow_slow_non_contiguous=True).then_inc(loaded, 16)
                loads.append(loaded)

            def column(ap):
                return ap.rearrange("(p o) -> p o", o=1)

            load(wxp_st, W_xp.rearrange("(k p) n -> p k n", p=P))
            load(lnb[:, 0:1], column(ln_b[0:P]))
            load(lnb[0:R, 1:2], column(ln_b[P:D]))
            load(win_st[0], W_in[0:P, :])
            load(win_st[1][0:R], W_in[P:D, :])
            load(win_st[1][R:P], W_in[P:D, :])
            load(wout_st[0], W_out[0:P, :])
            load(wout_st[1], W_out[P:D, :])
            load(wus_st, W_us)
            load(taps[:, :, :], W_conv.rearrange("(k p) o t -> p k (o t)", p=P))
            load(col[:, BIN:BIN + KE], b_in.rearrange("(k p) -> p k", p=P))
            load(col[:, BCV:BCV + KE], b_conv.rearrange("(k p) -> p k", p=P))
            load(col[:, SGB:SGB + 1], sg_b.rearrange("(p o) -> p o", o=1).broadcast_to([P, 1]))
            load(col[:, GA:GA + 1], column(ln_g[0:P]))
            load(col[0:R, GC:GC + 1], column(ln_g[P:D]))
            load(col[R:P, GC:GC + 1], column(ln_g[P:D]))
            load(wdt_st, W_dt.rearrange("(k p) n -> p k n", p=P))
            act.wait_ge(s_zeroed, 4)
            load(woutf_st[R:P, 1, :], W_out[D:2 * P, :])
            load(woutf_st[:, 2, :], W_out[2 * P:3 * P, :])
            load(col[:, USC:USC + 1], column(b_us[0:P]))
            load(col[0:R, USC + 1:USC + 2], column(b_us[P:D]))
            load(col[:, XPC:XPC + 1], column(b_xp[0:P]))
            load(col[0:R, XPC + 1:XPC + 2], column(b_xp[P:D]))
            load(bout_st[96:97, :], b_out.rearrange("(o d) -> o d", o=1))
            load(bout_st[97:98, :], b_out.rearrange("(o d) -> o d", o=1))
            for f in range(KE):
                act.wait_ge(s_prep_pe, f + 1)
                act.activation(wxpT[0][:, P * f:P * (f + 1)], gu[:, f, 0:P], ACT.Copy)
                act.activation(wxpT[1][:, P * f:P * (f + 1)], gu[0:R, f, P:2 * P], ACT.Copy).then_inc(s_prep_act, 1)
            for k, (c0, c1, at) in enumerate(((0, 8, 0), (8, 12, 0), (0, 4, 4), (4, 12, 0))):
                load(chan[PATCH * at:PATCH * (at + c1 - c0), k, :],
                     cw[c0:c1, :].unsqueeze(1).broadcast_to([c1 - c0, PATCH, D]), s_small)
            load(rt_st[:, 0, 0:NE], router_w[0:P, :], s_small)
            load(rt_st[:, 0, NE:NE + 1], sg_w[0:P, :], s_small)
            for half in range(2):
                load(rt_st[R * half:R * (half + 1), 1, 0:NE], router_w[P:D, :], s_small)
                load(rt_st[R * half:R * (half + 1), 1, NE:NE + 1], sg_w[P:D, :], s_small)
            for b in range(2):
                load(col[NST * b:NST * (b + 1), BDT:BDT + 1], column(b_dt), s_small)
                load(col[NST * b:NST * (b + 1), BDS:BDS + 1], column(b_xp[D:D + NST]), s_small)
            assert (loads.count(s_fold), loads.count(s_small)) == (FOLD_COUNT, SMALL_COUNT)

            act.wait_ge(s_const, 7)
            act.wait_ge(s_small, 16 * SMALL_COUNT)
            act.wait_ge(s_prep_w, 1)

            def weights_hi(n):
                act.wait_ge(s_stage[n % 3], piece_loaded(n))
                hi, _, w = piece_at(n)
                src = stage[n % 3][:, 0:w]
                if n >= 12:
                    src = src.rearrange("p (t d) -> p t d", d=D)
                act.activation(hi, src, ACT.Copy).then_inc(s_stage_hi, 1)

            def evac_pool(beta, b):
                wait(act, s_job["pool"], beta + 1)
                wait(act, s_hf, 2 * beta - 2)
                act.activation(h[0:TM, b, 0, :], bank("pool", b)[0:TM, 0:D], ACT.Copy)
                act.activation(h[0:IMG - TM, b, 1, :], bank("pool", b)[0:IMG - TM, D:2 * D], ACT.Copy).then_inc(s_tokens, 1)

            def double_tail(beta, norm, done, dst):
                wait(act, norm, beta + 1)
                act.activation(dst[0:TM, :, D:2 * P], dst[0:TM, :, P:D], ACT.Copy).then_inc(done, 1)

            def evac_hi(beta, b, name, dst, done):
                wait(act, s_job[name], beta + 1)
                act.activation(dst, bank(name, b)[:, 0:L], ACT.Copy).then_inc(done, 1)

            def evac_in(beta, b, e):
                k = 3 * beta + e
                wait(act, s_job["in"], k + 1)
                wait(act, s_actlo, k - 2)
                act.activation(xin[:, e, 3:3 + L], bank("in", b, e)[:, 0:L], ACT.Identity,
                               bias=binf[:, e:e + 1])
                act.activation(conv[:, e, :], bank("in", b, e)[:, 0:L], ACT.Identity, bias=bconv[:, e:e + 1],
                               scale=taps[:, e, 3:4]).then_inc(s_xin, 1)

            def silu_mix(beta, e):
                k = 3 * beta + e
                wait(act, s_tap, 3 * (k + 1))
                act.activation(xin[:, e, 3:3 + L], conv[:, e, :], ACT.Silu)
                if e == 0:
                    wait(act, s_job["act"], 2 * beta)
                act.activation(act_hi[:, e, :], conv[:, e, :], ACT.Silu).then_inc(s_acthi, 1)

            def evac_act(beta, b, k):
                wait(act, s_job["act"], 2 * beta + k + 1)
                if k == 0:
                    wait(act, s_zs, 2 * beta)
                    act.activation(yz[0:TM, 0:2, :], bank("act", b, 0)[0:TM, 0:2 * NX].rearrange("p (m n) -> p m n", m=2),
                                   ACT.Copy).then_inc(s_yz, 1)
                else:
                    act.activation(yz[0:TM, 2, :], bank("act", b, 1)[0:TM, 0:NX], ACT.Copy).then_inc(s_yz, 1)

            def scan_dt(q):
                wait(act, s_job["dt"], q + 1)
                act.activation(sc[0], bank("dt")[0:32, 0:L], ACT.Abs, bias=col[0:32, BDT:BDT + 1]).then_inc(s_exp1, 1)
                act.activation(sc[1], bank("dt")[0:32, 0:L], ACT.Relu, bias=col[0:32, BDT:BDT + 1]).then_inc(s_dtev, 1)

            def scan_ds(q):
                wait(act, s_job["ds"], q + 1)
                act.activation(sc[2], bank("ds")[0:32, 0:L], ACT.Identity, bias=col[0:32, BDS:BDS + 1]).then_inc(s_dsev, 1)

            def scan_exp(q):
                act.preload_act_table_set("natural_log_exp_and_others")
                wait(act, s_exp1, 2 * q + 1)
                act.activation(sc[0], sc[0], ACT.Exp, scale=-1.0).then_inc(s_exp1, 1)

            def scan_ln(q):
                wait(act, s_scan_w, q + 1)
                act.activation(sc[4], sc[3], ACT.Ln).then_inc(s_ln, 1)

            def scan_exp_half(q):
                wait(act, s_scan, SCAN_STEPS * q + 2)
                act.activation(sc[6], sc[6], ACT.Exp, scale=-0.5).then_inc(s_exp2, 1)

            def scan_tanh(q):
                wait(act, s_dtdone, q + 1)
                act.activation(sc[1], sc[4], ACT.Tanh, scale=0.5).then_inc(s_tanh1, 1)
                wait(act, s_kd, q + 1)
                act.activation(sc[3], sc[3], ACT.Tanh).then_inc(s_tanhk, 1)

            def us_hi(q):
                wait(act, s_usf, q + 1)
                act.activation(us[0:32, :], sc[1], ACT.Copy).then_inc(s_ushi, 1)
                act.activation(us[64:96, :], sc[1], ACT.Copy).then_inc(s_ushi, 1)

            def evac_mlp(beta):
                wait(act, s_down, T * (beta + 1))
                wait(act, s_job["mlpC"], min(beta + 2, 2 * NP) if isinstance(beta, int) else beta + 2)
                for part in range(2):
                    ins = act.activation(mlp_out[:, part, :], acc[:, part, 0:L], ACT.Copy)
                ins.then_inc(s_mlpout, 1)

            def gate_tanh(beta):
                wait(act, s_diff, beta + 1)
                act.activation(gsc[0:TM, 1, :], gsc[0:TM, 0, :], ACT.Tanh, scale=-0.5)
                act.activation(gsc[0:TM, 2, :], logit[0:TM, :, NE], ACT.Tanh, scale=0.5,
                               bias=sgbh[0:TM, :]).then_inc(s_gtanh, 1)

            def evac_gates(beta, b):
                wait(act, s_job["gates"], beta + 1)
                wait(act, s_gdram, 16 * beta)
                act.activation(gs[:, :], bank("gates", b)[0:NE + 1, 0:L], ACT.Copy).then_inc(s_gs, 1)

            def hidden_hi(i, s):
                n = SLOTS * i + s
                wait(act, s_hid, n + 1)
                wait(act, s_down, n - 2)
                act.activation(hid_hi[:, s % 3, :], hid[:, s % 3, :], ACT.Copy).then_inc(s_hi, 1)

            def silu_step(i, s):
                n = SLOTS * i + s
                wait(act, s_g, n + 1)
                wait(act, s_lo, n - 2)
                act.activation(hid[:, s % 3, :], gu[:, 2 * (s % 2), 0:L], ACT.Silu).then_inc(s_sil, 1)

            def step(name, b, k, q):
                beta = 2 * q + b
                if name == "pool":
                    evac_pool(beta, b)
                elif name == "double":
                    double_tail(beta, s_norm, s_dup, xn)
                elif name == "doublef":
                    double_tail(beta, s_normf, s_dupf, xnf)
                elif name == "mixA":
                    wait(act, s_job["in"], 3 * beta)
                    evac_hi(beta, b, "mixA", mixA_hi[:, :], s_mixhi)
                elif name == "mixC":
                    evac_hi(beta, b, "mixC", mixC[:, :], s_mixc0)
                elif name == "in":
                    evac_in(beta, b, k)
                elif name == "convsilu":
                    silu_mix(beta, k)
                elif name == "act":
                    evac_act(beta, b, k)
                elif name == "dt":
                    scan_dt(q)
                elif name == "ds":
                    scan_ds(q)
                elif name == "exp":
                    scan_exp(q)
                elif name == "ln":
                    scan_ln(q)
                elif name == "exp2":
                    scan_exp_half(q)
                elif name == "tanh":
                    scan_tanh(q)
                elif name == "states":
                    us_hi(q)
                elif name == "mlpA":
                    wait(act, s_u, T * (beta - 1))
                    evac_hi(beta, b, "mlpA", mlpA_hi[:, b, :], s_mlphi)
                elif name == "mlpC":
                    evac_hi(beta, b, "mlpC", mlpC[:, b, :], s_mlpc0)
                elif name == "out":
                    evac_mlp(beta)
                elif name == "gtanh":
                    gate_tanh(beta)
                elif name == "gates":
                    evac_gates(beta, b)
                else:
                    raise AssertionError(name)

            def iteration(i, mlp, carry, mix, pooling):
                for s in range(SLOTS):
                    for name, b, k in steps(ACT_STEPS, s):
                        if name == "silu":
                            if mlp:
                                silu_step(i, s)
                        elif name == "hi":
                            if mlp and s > 0:
                                hidden_hi(i, s - 1)
                            elif carry:
                                hidden_hi(i - 1, SLOTS - 1)
                        elif pair_of(i, name, b, carry, mlp, mix) is not None:
                            step(name, b, k, pair_of(i, name, b, carry, mlp, mix))
                    if isinstance(i, int) and i == -1 and s < PIECES:
                        weights_hi(s)

            iterations(act, iteration, FULL)
            hidden_hi(NP - 1, SLOTS - 1)
            evac_mlp(2 * NP - 1)

        @block.vector
        def _(dve):
            def weights_lo(n):
                dve.wait_ge(s_stage_hi, n + 1)
                _, _, w = piece_at(n)
                src = stage[n % 3][:, 0:w]
                if n >= 12:
                    src = src.rearrange("p (t d) -> p t d", d=D)
                for hi, lo, c in pieces_of_lo(n):
                    ins = dve.tensor_tensor(lo, src[:, :, c] if n >= 12 else src, hi.bitcast(F32), ALU.subtract)
                ins.then_inc(s_stage_lo, 1)

            def pool_chunk(q, c):
                tile, j = divmod(c, G // 2)
                wait(dve, s_chunk[c % RING], 32 * (3 * q + tile + 1))
                if j == 0:
                    wait(dve, s_job["pool"], 2 * q)
                dve.tensor_reduce(pooled[:, tile, 2 * G * j:2 * G * (j + 1)],
                                  ring[:, c % RING, :].rearrange("p (t k) -> p t k", k=PATCH), AX_X,
                                  ALU.add).then_inc(s_pooled, 1)

            def settle(s, value):
                wait(dve, s, value)
                dve.memset(settled[:, :], 0.0)

            def stats_of(beta, b, k, src, chain_sem, aggregated, done, slope, offset):
                for m in range(3):
                    ins = dve.bn_stats(stats[0:TM, k, m, :], src[0:TM, b, m, :])
                ins.then_inc(chain_sem, 1)
                settle(chain_sem, beta + 1)
                for m in range(3):
                    ins = dve.bn_aggr(mv[0:TM, k, m, :], stats[0:TM, k, m, :])
                ins.then_inc(aggregated, 1)
                wait(dve, aggregated, beta + 1)
                dve.tensor_scalar(rstd[0:TM, k, :], mv[0:TM, k, :, 1], slope, offset, ALU.mult, ALU.add).then_inc(done, 1)

            def normalise(beta, b, k, src, dst, ready, done, own):
                wait(dve, ready, beta + 1)
                wait(dve, own, beta + 1)
                for m in range(3):
                    ins = dve.tensor_scalar(dst[0:TM, m, 0:D], src[0:TM, b, m, :], mv[0:TM, k, m, 0:1],
                                            rstd[0:TM, k, m:m + 1], ALU.subtract, ALU.mult)
                ins.then_inc(done, 1)

            def split_A(beta, src, hi_ready, hi, lo, done):
                wait(dve, hi_ready, beta + 1)
                dve.tensor_tensor(lo, src[:, 0:L], hi.bitcast(F32), ALU.subtract).then_inc(done, 1)

            def split_C(beta, src, hi_ready, both, done):
                wait(dve, hi_ready, beta + 1)
                dve.tensor_tensor(both[64:P], src[64:P, 0:L], both[64:P].bitcast(F32), ALU.subtract).then_inc(done, 1)

            def conv_taps(beta, e):
                k = 3 * beta + e
                wait(dve, s_xin, k + 1)
                for j in range(3):
                    if j:
                        wait(dve, s_tap, 3 * k + j)
                    dve.scalar_tensor_tensor(conv[:, e, :], xin[:, e, 2 - j:2 - j + L], taps[:, e, 2 - j:3 - j],
                                             conv[:, e, :], ALU.mult, ALU.add).then_inc(s_tap, 1)

            def act_lo_of(beta, e):
                wait(dve, s_acthi, 3 * beta + e + 1)
                dve.tensor_tensor(act_lo[:, e, :], xin[:, e, 3:3 + L], act_hi[:, e, :].bitcast(F32),
                                  ALU.subtract).then_inc(s_actlo, 1)

            def scan_1(q, part):
                base = SCAN_STEPS * q
                if part == 0:
                    wait(dve, s_exp1, 2 * q + 2)
                    dve.tensor_scalar(sc[3], sc[0], 1.0, None, ALU.add).then_inc(s_scan_w, 1)
                    wait(dve, s_scan_w, q + 1)
                    dve.scalar_tensor_tensor(sc[5], sc[3], -1.0, sc[0], ALU.add, ALU.subtract).then_inc(s_scan, 1)
                    return
                wait(dve, s_ln, q + 1)
                wait(dve, s_dtev, q + 1)
                dve.tensor_tensor(sc[6], sc[4], sc[1], ALU.add).then_inc(s_scan, 1)
                wait(dve, s_scan, base + 1)
                dve.tensor_tensor(sc[3], sc[4], sc[5], ALU.subtract).then_inc(s_scan, 1)
                wait(dve, s_scan, base + 3)
                dve.scalar_tensor_tensor(sc[3], sc[0], 0.69, sc[3], ALU.mult, ALU.max).then_inc(s_scan, 1)
                wait(dve, s_scan, base + 4)
                dve.tensor_tensor(sc[4], sc[3], sc[1], ALU.add).then_inc(s_dtdone, 1)
                wait(dve, s_dtdone, q + 1)
                dve.tensor_tensor(sc[3], sc[4], khalf[:, :], ALU.mult).then_inc(s_kd, 1)

            def scan_2(q, part):
                base = SCAN_STEPS * q + 4
                if part == 0:
                    wait(dve, s_ab, 2 * q + 2)
                    dve.tensor_tensor_scan(sc[6], sc[5], sc[2], 0.0, ALU.mult, ALU.add).then_inc(s_scan, 1)
                    wait(dve, s_tanh1, q + 1)
                    wait(dve, s_tanhk, q + 1)
                    dve.tensor_scalar(sc[4], sc[1], 2.0, 1e-30, ALU.mult, ALU.max).then_inc(s_scan, 1)
                    wait(dve, s_scan, base + 2)
                    dve.scalar_tensor_tensor(sc[0], sc[3], 1.0, sc[4], ALU.add, ALU.mult).then_inc(s_scan, 1)
                    dve.scalar_tensor_tensor(sc[1], sc[1], 1.0, sc[2], ALU.add, ALU.mult).then_inc(s_scan, 1)
                elif part == 1:
                    wait(dve, s_scan, base + 3)
                    dve.reciprocal(sc[0], sc[0]).then_inc(s_scan, 1)
                elif part == 2:
                    wait(dve, s_scan, base + 4)
                    dve.scalar_tensor_tensor(sc[1], sc[3], 2.0, sc[1], ALU.mult, ALU.mult).then_inc(s_scan, 1)
                    wait(dve, s_scan, base + 5)
                    dve.tensor_tensor(sc[4], sc[4], sc[0], ALU.mult).then_inc(s_scan, 1)
                    wait(dve, s_scan, base + 6)
                    dve.tensor_tensor(sc[1], sc[1], sc[0], ALU.mult).then_inc(s_scan, 1)
                    wait(dve, s_scan, base + 7)
                    dve.scalar_tensor_tensor(sc[3], sc[3], -1.0, sc[4], ALU.add, ALU.mult).then_inc(s_scan, 1)
                else:
                    wait(dve, s_scan, base + 9)
                    dve.tensor_tensor(sc[3], sc[3], sc[6], ALU.mult).then_inc(s_scan, 1)
                    wait(dve, s_scan, base + 10)
                    dve.tensor_tensor(sc[1], sc[1], sc[3], ALU.subtract).then_inc(s_usf, 1)

            def us_lo(q):
                wait(dve, s_ushi, 2 * q + 1)
                dve.tensor_tensor(us[32:64, :], sc[1], us[0:32, :].bitcast(F32), ALU.subtract).then_inc(s_uslo, 1)

            def evac_us(beta, b, k):
                wait(dve, s_job["us"], 2 * beta + k + 1)
                wait(dve, s_hy, 2 * beta + k + 1)
                m = slice(0, 2) if k == 0 else slice(2, 3)
                n = 2 if k == 0 else 1
                dve.tensor_tensor(hf[0:TM, b, m, :], bank("us", b, k)[0:TM, 0:n * D].rearrange("p (m d) -> p m d", m=n),
                                  h[0:TM, b, m, :], ALU.add).then_inc(s_hf, 1)

            def evac_route(beta, b):
                wait(dve, s_job["route"], beta + 1)
                dve.tensor_copy(lg[0:TM, :, :], bank("route", b)[0:TM, 0:96].rearrange("p (m n) -> p m n", m=3)).then_inc(s_lg, 1)

            GATE_STEPS = 8

            def gates_1(beta):
                base = GATE_STEPS * beta
                wait(dve, s_lg, beta + 1)
                dve.tensor_tensor(logit[0:TM, :, :], lg[0:TM, :, 0:16], lg[0:TM, :, 16:32], ALU.add).then_inc(s_gate, 1)
                settle(s_gate, base + 1)
                for m in range(3):
                    ins = dve.max(top[0:TM, m, :], logit[0:TM, m, 0:NE])
                ins.then_inc(s_gate, 1)
                wait(dve, s_gate, base + 2)
                dve.tensor_tensor(gsc[0:TM, 0, :], top[0:TM, :, 1], top[0:TM, :, 0], ALU.subtract).then_inc(s_diff, 1)
                for m in range(3):
                    ins = dve.max_index(topi[0:TM, m, :], top[0:TM, m, :], logit[0:TM, m, 0:NE])
                ins.then_inc(s_gate, 1)
                wait(dve, s_gate, base + 3)
                dve.tensor_copy(topf[0:TM, :, :], topi[0:TM, :, :]).then_inc(s_gate, 1)
                wait(dve, s_gate, base + 4)
                for r in range(2):
                    ins = dve.tensor_tensor(pick[0:TM, r, :, :],
                                            biota[0:TM, :].unsqueeze(1).broadcast_to([TM, 3, NE]),
                                            topf[0:TM, :, r:r + 1].broadcast_to([TM, 3, NE]), ALU.is_equal)
                ins.then_inc(s_gate, 1)

            def gates_2(beta):
                base = GATE_STEPS * beta + 5
                wait(dve, s_gtanh, beta + 1)
                g = gsc[0:TM, :, :]
                dve.tensor_scalar(g[:, 3, :], g[:, 1, :], 0.5, 0.5, ALU.mult, ALU.add)
                dve.tensor_scalar(g[:, 4, :], g[:, 1, :], -0.5, 0.5, ALU.mult, ALU.add)
                dve.tensor_scalar(g[:, 5, :], g[:, 2, :], -0.5, 0.5, ALU.mult, ALU.add)
                dve.tensor_scalar(gt[0:TM, :, NE], g[:, 2, :], 0.5, 0.5, ALU.mult, ALU.add).then_inc(s_gate, 1)
                wait(dve, s_gate, base + 1)
                dve.tensor_tensor(g[:, 6, :], g[:, 3, :], g[:, 5, :], ALU.mult)
                dve.tensor_tensor(g[:, 7, :], g[:, 4, :], g[:, 5, :], ALU.mult).then_inc(s_gate, 1)
                wait(dve, s_gate, base + 2)
                for r in range(2):
                    ins = dve.tensor_tensor(pick[0:TM, r, :, :], pick[0:TM, r, :, :],
                                            g[:, 6 + r, :].unsqueeze(2).broadcast_to([TM, 3, NE]), ALU.mult)
                ins.then_inc(s_gate, 1)
                wait(dve, s_gate, base + 3)
                dve.tensor_tensor(gt[0:TM, :, 0:NE], pick[0:TM, 0, :, :], pick[0:TM, 1, :, :], ALU.add).then_inc(s_gt, 1)

            def hidden(i, s):
                n = SLOTS * i + s
                wait(dve, s_u, n + 1)
                wait(dve, s_gated, n + 1)
                dve.tensor_tensor(hid[:, s % 3, :], gu[:, 2 * (s % 2) + 1, 0:L], hid[:, s % 3, :], ALU.mult).then_inc(s_hid, 1)

            def hidden_lo(i, s):
                n = SLOTS * i + s
                wait(dve, s_hi, n + 1)
                wait(dve, s_down, n - 2)
                dve.tensor_tensor(hid_lo[:, s % 3, :], hid[:, s % 3, :], hid_hi[:, s % 3, :].bitcast(F32),
                                  ALU.subtract).then_inc(s_lo, 1)

            def result(beta, b, k):
                wait(dve, s_job["out"], 2 * beta + k + 1)
                if k == 0:
                    wait(dve, s_out, 16 * beta)
                m, n = (slice(2, 3), 1) if k else (slice(0, 2), 2)
                src = bank("out", b, k)[0:TM, 0:2 * P * n].rearrange("p (m c) -> p m c", m=n)
                dve.tensor_tensor(res[0:TM, m, :], src[:, :, 0:D], hf[0:TM, b, m, :], ALU.add).then_inc(s_res1, 1)
                wait(dve, s_res1, 2 * beta + k + 1)
                dve.tensor_tensor(res[0:TM, m, P:D], src[:, :, D:2 * P], res[0:TM, m, P:D], ALU.add).then_inc(s_res, 1)

            def step(name, b, k, q):
                beta = 2 * q + b
                if name == "stats":
                    wait(dve, s_tokens, beta + 1)
                    wait(dve, s_txt[b], 32 * (q + 1))
                    stats_of(beta, b, b, h, s_stat, s_mv, s_rstd_a, 1.0 + EPS, EPS * EPS)
                elif name == "norm":
                    normalise(beta, b, b, h, xn, s_rstd, s_norm, s_mv)
                elif name == "statsf":
                    wait(dve, s_hf, 2 * beta + 2)
                    stats_of(beta, b, 2 + b, hf, s_statf, s_mvf, s_rstdf_a, 1.0, EPS)
                elif name == "normf":
                    wait(dve, s_job["out"], 2 * (beta - 1))
                    normalise(beta, b, 2 + b, hf, xnf, s_rstdf, s_normf, s_mvf)
                elif name == "mixA":
                    split_A(beta, bank(name, b), s_mixhi, mixA_hi[:, :], mixA_lo[:, :], s_mixlo)
                elif name == "mixC":
                    split_C(beta, bank(name, b), s_mixc0, mixC, s_mixc)
                elif name == "result":
                    result(beta, b, k)
                elif name == "conv":
                    conv_taps(beta, k)
                elif name == "actlo":
                    act_lo_of(beta, k)
                elif name == "softplus":
                    scan_1(q, k)
                elif name == "scan":
                    scan_2(q, k)
                elif name == "stateslo":
                    us_lo(q)
                elif name == "us":
                    evac_us(beta, b, k)
                elif name == "mlpA":
                    split_A(beta, bank(name, b), s_mlphi, mlpA_hi[:, b, :], mlpA_lo[:, b, :], s_mlplo)
                elif name == "mlpC":
                    split_C(beta, bank(name, b), s_mlpc0, mlpC[:, b, :], s_mlpc)
                elif name == "route":
                    evac_route(beta, b)
                elif name == "pick":
                    gates_1(beta)
                elif name == "weigh":
                    gates_2(beta)
                else:
                    raise AssertionError(name)

            def iteration(i, mlp, carry, mix, pooling):
                for s in range(SLOTS):
                    for name, b, k in steps(DVE_STEPS, s):
                        if name in ("hidden", "lo"):
                            work = hidden if name == "hidden" else hidden_lo
                            if mlp and s > 0:
                                work(i, s - 1)
                            elif carry:
                                work(i - 1, SLOTS - 1)
                        elif name == "pool":
                            if pooling:
                                pool_chunk(i + 2, k)
                        elif pair_of(i, name, b, carry, mlp, mix) is not None:
                            step(name, b, k, pair_of(i, name, b, carry, mlp, mix))
                    if isinstance(i, int) and i == -1 and s < PIECES:
                        weights_lo(s)

            for c in range(POOL_BEFORE):
                pool_chunk(0, c)
            chained = [0]

            def chain(ins):
                chained[0] += 1
                ins.then_inc(s_prep_dve, 1)
                dve.wait_ge(s_prep_dve, chained[0])

            dve.wait_ge(s_fold, 16 * FOLD_COUNT)
            dve.wait_ge(s_const, 7)
            chain(dve.memset(us[96:128, :].bitcast(F32), 1.0))
            dve.wait_ge(s_prep_pe, 4)
            chain(dve.tensor_tensor(binf[:, :], prep[:, 0:KE], col[:, BIN:BIN + KE], ALU.add))
            chain(dve.tensor_tensor(bconv[:, :], binf[:, :], taps[:, :, 3], ALU.mult))
            chain(dve.tensor_tensor(bconv[:, :], bconv[:, :], col[:, BCV:BCV + KE], ALU.add))
            chain(dve.tensor_scalar(sgbh[:, :], col[:, SGB:SGB + 1], 0.5, None, ALU.mult))
            for st, g, hi, lo in ((win_st[0], GA, inA_hi, inA_lo), (win_st[1], GC, inC_hi, inC_lo)):
                chain(dve.tensor_scalar(st, st, col[:, g:g + 1], None, ALU.mult))
                chain(dve.tensor_copy(hi[:, :], st))
                chain(dve.tensor_tensor(lo[:, :], st, hi[:, :].bitcast(F32), ALU.subtract))
            for f in range(KE):
                dve.wait_ge(s_prep_pe, 5 + f)
                full = wx_full[:, f, :]
                chain(dve.tensor_tensor(full[:, 0:D], gu[:, f, 0:D], woutf_st[:, f, :], ALU.add))
                chain(dve.tensor_copy(full[:, D:D + NST], wdt_st[:, f, :]))
                chain(dve.tensor_copy(full[:, D + NST:NX], wxp_st[:, f, D:D + NST]))
                chain(dve.tensor_copy(actw_hi[:, f, :], full))
                chain(dve.tensor_tensor(actw_lo[:, f, :], full, actw_hi[:, f, :].bitcast(F32), ALU.subtract))
            dve.wait_ge(s_prep_pe, 8)
            for part, rows in ((0, P), (1, R)):
                chain(dve.memset(uslT[part][:, :, :], 0.0))
                for b in range(2):
                    for q in range(3):
                        at = 32 * q + NST * b
                        chain(dve.tensor_copy(uslT[part][:, b, at:at + NST], prep[0:rows, NST * part:NST * (part + 1)]))
                    for c in (96, 97):
                        ins = dve.tensor_tensor(uslT[part][:, b, c:c + 1], col[0:rows, USC + part:USC + part + 1],
                                                col[0:rows, XPC + part:XPC + part + 1], ALU.add)
            ins.then_inc(s_usl, 1)
            for b in range(2):
                dve.wait_ge(s_prep_pe, 9 + b)
                chain(dve.tensor_tensor(uw, acc[:, b, 0:D], bout_st, ALU.add))
                chain(dve.tensor_copy(usw[:, b, :], uw))
                chain(dve.tensor_tensor(uw, uw, usw[:, b, :].bitcast(F32), ALU.subtract))
                chain(dve.tensor_scalar(uw, uw, col[:, MLO:MLO + 1], None, ALU.mult))
                chain(dve.scalar_tensor_tensor(usw[:, b, :], usw[:, b, :].bitcast(F32), col[:, MHI:MHI + 1], uw,
                                               ALU.mult, ALU.add))
            for c in range(POOL_BEFORE, CHUNKS):
                pool_chunk(0, c)
            dve.wait_ge(s_small, 16 * SMALL_COUNT)
            for part, w in ((0, routeA), (1, routeC)):
                chain(dve.tensor_copy(w[:, 0:16], rt_st[:, part, :]))
                ins = dve.tensor_tensor(w[:, 16:32], rt_st[:, part, :], w[:, 0:16].bitcast(F32), ALU.subtract)
            ins.then_inc(s_prep_w, 1)

            iterations(dve, iteration, FULL)
            hidden(NP - 1, SLOTS - 1)
            hidden_lo(NP - 1, SLOTS - 1)
            for k in range(2):
                result(2 * NP - 1, 1, k)

        @block.tensor
        def _(pe):
            def mm(dst, w, m, start, stop):
                return nc.tensor.matmul(dst, w, m, start=start, stop=stop)

            pe.wait_ge(s_fold, 16 * FOLD_COUNT)
            pe.wait_ge(s_const, 1)
            for f in range(KE):
                nc.tensor.transpose(gu[:, f, 0:P], wxp_st[:, f, 0:P], ident[:, :])
                nc.tensor.transpose(gu[0:R, f, P:2 * P], wxp_st[:, f, P:D], ident[:, :]).then_inc(s_prep_pe, 1)
            for e in range(KE):
                mm(prep[:, e:e + 1], win_st[0][:, P * e:P * (e + 1)], lnb[:, 0:1], True, False)
                last = mm(prep[:, e:e + 1], win_st[1][0:R, P * e:P * (e + 1)], lnb[0:R, 1:2], False, True)
            last.then_inc(s_prep_pe, 1)
            pe.wait_ge(s_prep_act, KE)
            for f in range(KE):
                mm(gu[:, f, 0:D], wxpT[0][:, P * f:P * (f + 1)], wout_st[0], True, False)
                mm(gu[:, f, 0:D], wxpT[1][:, P * f:P * (f + 1)], wout_st[1], False, True).then_inc(s_prep_pe, 1)
            pe.wait_ge(s_prep_dve, 2)
            nc.tensor.transpose(prep[:, 0:NST], wus_st[:, 0:P], ident[0:NST, 0:NST])
            nc.tensor.transpose(prep[0:R, NST:2 * NST], wus_st[:, P:D], ident[0:NST, 0:NST]).then_inc(s_prep_pe, 1)
            pe.wait_ge(s_usl, 1)
            for b in range(2):
                mm(acc[:, b, 0:D], uslT[0][:, b, :], wout_st[0], True, False)
                mm(acc[:, b, 0:D], uslT[1][:, b, :], wout_st[1], False, True).then_inc(s_prep_pe, 1)
            pe.wait_ge(s_prep_w, 1)

            def up_step(i, s, k):
                n, b, t = SLOTS * i + s, s // T, s % T
                if k == 0:
                    if t == 0:
                        wait(pe, s_mlplo, 2 * i + b + 1)
                        wait(pe, s_mlpc, 2 * i + b + 1)
                    wait(pe, s_sil, n - 1)
                else:
                    wait(pe, s_hid, n - 1)
                at, done = ((gate_col(t), s_g), (up_col(t), s_u))[k]
                dst = gu[:, 2 * (s % 2) + k, 0:L]
                c = slice(at, at + P)
                mm(dst, upA_hi[:, c], mlpA_hi[:, b, :], True, False)
                mm(dst, upA_lo[:, c], mlpA_hi[:, b, :], False, False)
                mm(dst, upA_hi[:, c], mlpA_lo[:, b, :], False, False)
                mm(dst, upC_hi[:, c], mlpC[:, b, :], False, False)
                mm(dst, upC_lo[:, c], mlpC[:, b, :], False, True).then_inc(done, 1)

            def down_step(i, s):
                n, t = SLOTS * i + s, s % T
                hi, lo = hid_hi[:, s % 3, :], hid_lo[:, s % 3, :]
                wait(pe, s_hi, n + 1)
                if t == 0:
                    wait(pe, s_mlpout, 2 * i + s // T)
                A, C, first, end = acc[:, 0, 0:L], acc[:, 1, 0:L], t == 0, t == T - 1
                mm(A, down[:, t, 0:P], hi, first, False)
                mm(A, down[:, t, P + 2 * R:2 * D], hi, False, False)
                if not end:
                    mm(C, down[:, t, P:2 * P], hi, first, False)
                wait(pe, s_lo, n + 1)
                mm(A, down[:, t, 0:P], lo, False, end)
                last = mm(C[0:R], down[:, t, P:D], lo, False, False)
                if end:
                    last = mm(C, down[:, t, P:2 * P], hi, False, True)
                last.then_inc(s_down, 1)

            def transposes(dst, src, at):
                for m in range(3):
                    last = nc.tensor.transpose(dst[:, TM * m:TM * (m + 1)], src[0:TM, m, at:at + P], ident[0:TM, 0:TM])
                return last

            def job(name, b, k, q):
                beta = 2 * q + b
                to = bank(name, b, k)
                if name == "pool":
                    wait(pe, s_pooled, CHUNKS * (q + 1))
                    for m, (t0, t1) in enumerate(((0, TM), (TM, IMG))):
                        dst = to[0:t1 - t0, D * m:D * (m + 1)]
                        mm(dst, pooled[:, b, t0:t1], chan[:, 2 * b, :], True, False)
                        last = mm(dst, pooled[:, b + 1, t0:t1], chan[:, 2 * b + 1, :], False, True)
                    last.then_inc(s_job["pool"], 1)
                elif name in ("mixA", "mixC"):
                    wait(pe, s_dup, beta + 1)
                    transposes(to, xn, 0 if name == "mixA" else P).then_inc(s_job[name], 1)
                elif name in ("mlpA", "mlpC"):
                    wait(pe, s_dupf, beta + 1)
                    transposes(to, xnf, 0 if name == "mlpA" else P).then_inc(s_job[name], 1)
                elif name == "in":
                    if k == 0:
                        wait(pe, s_mixlo, beta + 1)
                        wait(pe, s_mixc, beta + 1)
                    c = slice(P * k, P * (k + 1))
                    dst = to[:, 0:L]
                    mm(dst, inA_hi[:, c], mixA_hi[:, :], True, False)
                    mm(dst, inA_lo[:, c], mixA_hi[:, :], False, False)
                    mm(dst, inA_hi[:, c], mixA_lo[:, :], False, False)
                    mm(dst, inC_hi[:, c], mixC[:, :], False, False)
                    mm(dst, inC_lo[:, c], mixC[:, :], False, True).then_inc(s_job["in"], 1)
                elif name == "act":
                    wait(pe, s_actlo, 3 * beta + 3)
                    for at, m in enumerate((2,) if k else (0, 1)):
                        tok = slice(TM * m, TM * (m + 1))
                        dst = to[0:TM, NX * at:NX * (at + 1)]
                        for f in range(KE):
                            mm(dst, act_hi[:, f, tok], actw_hi[:, f, :], f == 0, False)
                            mm(dst, act_hi[:, f, tok], actw_lo[:, f, :], False, False)
                            last = mm(dst, act_lo[:, f, tok], actw_hi[:, f, :], False, f == KE - 1)
                    last.then_inc(s_job["act"], 1)
                elif name in ("dt", "ds"):
                    wait(pe, s_zs, 4 * (q + 1))
                    at = 0 if name == "dt" else 2 * NST
                    for m in range(3):
                        last = nc.tensor.transpose(to[0:2 * NST, TM * m:TM * (m + 1)], zs[0:TM, m, at:at + 2 * NST],
                                                   ident[0:TM, 0:TM])
                    last.then_inc(s_job[name], 1)
                elif name == "us":
                    wait(pe, s_uslo, q + 1)
                    wait(pe, s_ushi, 2 * q + 2)
                    for at, m in enumerate((2,) if k else (0, 1)):
                        last = mm(to[0:TM, D * at:D * (at + 1)], us[:, TM * m:TM * (m + 1)], usw[:, b, :], True, True)
                    last.then_inc(s_job["us"], 1)
                elif name == "route":
                    wait(pe, s_mlplo, beta + 1)
                    wait(pe, s_mlpc, beta + 1)
                    for m in range(3):
                        tok = slice(TM * m, TM * (m + 1))
                        dst = to[0:TM, 32 * m:32 * (m + 1)]
                        mm(dst, mlpA_hi[:, b, tok], routeA[:, :], True, False)
                        mm(dst[:, 0:16], mlpA_lo[:, b, tok], routeA[:, 0:16], False, False)
                        last = mm(dst, mlpC[:, b, tok], routeC[:, :], False, True)
                    last.then_inc(s_job["route"], 1)
                elif name == "out":
                    wait(pe, s_mlpout, beta + 1)
                    for at, m in enumerate((2,) if k else (0, 1)):
                        for part in range(2):
                            last = nc.tensor.transpose(to[0:TM, P * (2 * at + part):P * (2 * at + part + 1)],
                                                       mlp_out[:, part, TM * m:TM * (m + 1)], ident[:, :])
                    last.then_inc(s_job["out"], 1)
                elif name == "gates":
                    wait(pe, s_gt, beta + 1)
                    for m in range(3):
                        last = nc.tensor.transpose(to[0:NE + 1, TM * m:TM * (m + 1)], gt[0:TM, m, :], ident[0:TM, 0:TM])
                    last.then_inc(s_job["gates"], 1)

                else:
                    raise AssertionError(name)

            def wait_for_bank(i, now, carry, mlp, mix):
                at = JOBS.index(now)
                earlier = [(j, i, (carry, mlp, mix)) for j in reversed(JOBS[at % 2:at:2])]
                before = parts(i - 1) if isinstance(i, int) else parts(1)
                earlier += [(j, i - 1, (before["carry"], before["mlp"], before["mix"])) for j in reversed(JOBS[at % 2::2])]
                for (name, b, k), of, has in earlier:
                    q = pair_of(of, name, b, *has)
                    if q is not None:
                        wait(pe, *evacuated(name, b, k, q))
                        return

            def iteration(i, mlp, carry, mix, pooling):
                for s in range(SLOTS):
                    for name, b, k in steps(PE_STEPS, s):
                        if name in ("gate", "up"):
                            if mlp:
                                up_step(i, s, int(name == "up"))
                        elif name == "down":
                            if mlp and s >= 2:
                                down_step(i, s - 2)
                            elif carry:
                                down_step(i - 1, SLOTS - 2 + s)
                        elif pair_of(i, name, b, carry, mlp, mix) is not None:
                            wait_for_bank(i, (name, b, k), carry, mlp, mix)
                            job(name, b, k, pair_of(i, name, b, carry, mlp, mix))
                if isinstance(i, int) and i == -1:
                    pe.wait_ge(s_stage_lo, PIECES)

            iterations(pe, iteration, FULL)
            down_step(NP - 1, SLOTS - 2)
            down_step(NP - 1, SLOTS - 1)
            for k in range(2):
                wait_for_bank(NP, ("out", 1, k), False, False, False)
                job("out", 1, k, NP - 1)


_OUT = ((64, 324, 192), "float32")
_INS = ["x", "txt", "L0_tok_channel_weights"] + ["L0_attn_" + n for n in (
    "ln_g", "ln_b", "W_in", "b_in", "W_conv", "b_conv", "W_xp", "b_xp", "W_dt", "b_dt", "W_us", "b_us", "W_out", "b_out")] + [
    "L0_ffn_" + n for n in ("router_w", "w_gate", "w_up", "w_down", "ws_gate", "ws_up", "ws_down", "sg_w", "sg_b")]


def kernel(**inputs):
    import numpy as _np
    import concourse.bacc as _bacc
    from concourse import mybir as _mybir
    from concourse.bass_utils import run_bass_kernel_spmd as _run

    nc = _bacc.Bacc("TRN2", target_bir_lowering=False, num_devices=1)
    arrays, args = {}, []
    for name in _INS:
        a = _np.ascontiguousarray(inputs[name])
        arrays[f"in_{name}_dram"] = a
        args.append(nc.dram_tensor(f"in_{name}_dram", a.shape, _mybir.dt.from_np(a.dtype), kind="ExternalInput").ap())
    shape = (inputs["x"].shape[0],) + _OUT[0][1:]
    result = nc.dram_tensor("out_0_dram", shape, _mybir.dt.from_np(_np.dtype(_OUT[1])), kind="ExternalOutput").ap()
    build(nc, *args, result)
    r = _run(nc, [arrays], core_ids=[0])
    return r.results[0]["out_0_dram"]
```
